# Optimizing a Trainium2 kernel written in Bass

```python
import numpy as np
import jax
import jax.numpy as jnp

def _softmax(x, axis=-1):
    return jax.nn.softmax(x, axis=axis)
def _gelu(x):
    return jax.nn.gelu(x, approximate=True)
def _silu(x):
    return jax.nn.silu(x)
def _sigmoid(x):
    return jax.nn.sigmoid(x)
def _layernorm(x, axis=-1, eps=1e-5):
    m = jnp.mean(x, axis=axis, keepdims=True)
    v = jnp.var(x, axis=axis, keepdims=True)
    return (x - m) / jnp.sqrt(v + eps)
def _scatter_add(tgt, idx, src, axis=0):
    return tgt.at[idx].add(src)
def _segment_sum(src, seg, n):
    return jax.ops.segment_sum(src, seg, n)

kernel_name = 'mk_conv_preact_d1_conv_nchw64_a08ee5'

def setup_inputs(seed: int = 0):
    np.random.seed(seed)
    _w = jnp.asarray
    def _rec_inputs():
        import jax
        import jax.numpy as jnp
        _gk = jax.random.key(seed)
        x = 7.22e-05 + 1 * jax.random.normal(jax.random.fold_in(_gk, 1), (2, 64, 256, 256), jnp.float32)
        return x
    x = _rec_inputs()
    def _L0_conv_setup():
        import jax, jax.numpy as jnp
        import numpy as np
        from jax import lax
        HEADS = 8
        DIM_HEAD = 64
        EPS = 1e-12

        def _l2norm(t):
            n = jnp.sqrt(jnp.sum(t * t, axis=-1, keepdims=True))
            return t / jnp.maximum(n, EPS)
        key = jax.random.key(seed)
        ks = jax.random.split(key, 7)
        b, c, h, w = (2, 64, 256, 256)
        inner = HEADS * DIM_HEAD
        return {'x_in': jax.random.normal(ks[0], (b, c, h, w), jnp.float32), 'Wq': jax.random.normal(ks[1], (c, inner), jnp.float32) * 0.02, 'Wk': jax.random.normal(ks[2], (c, inner), jnp.float32) * 0.02, 'Wv': jax.random.normal(ks[3], (c, inner), jnp.float32) * 0.02, 'rescale': jnp.ones((HEADS, 1, 1), jnp.float32), 'Wp': jax.random.normal(ks[4], (inner, c), jnp.float32) * 0.02, 'bp': jnp.zeros((c,), jnp.float32), 'pos_k': jax.random.normal(ks[5], (c, 1, 3, 3), jnp.float32) * 0.1}
    _L0_conv_all = _L0_conv_setup()
    _L0_conv_in = {k: v for k, v in _L0_conv_all.items() if k in ('Wq', 'Wk', 'Wv', 'rescale', 'Wp', 'bp', 'pos_k', )}
    del _L0_conv_all

    return {
        "x": x,
        "L0_conv_Wq": _L0_conv_in["Wq"],
        "L0_conv_Wk": _L0_conv_in["Wk"],
        "L0_conv_Wv": _L0_conv_in["Wv"],
        "L0_conv_rescale": _L0_conv_in["rescale"],
        "L0_conv_Wp": _L0_conv_in["Wp"],
        "L0_conv_bp": _L0_conv_in["bp"],
        "L0_conv_pos_k": _L0_conv_in["pos_k"],
    }

def reference(x, L0_conv_Wq, L0_conv_Wk, L0_conv_Wv, L0_conv_rescale, L0_conv_Wp, L0_conv_bp, L0_conv_pos_k):
    import jax
    import jax.numpy as jnp
    def _L0_conv_ref(x_in, Wq, Wk, Wv, rescale, Wp, bp, pos_k):
        import jax, jax.numpy as jnp
        import numpy as np
        from jax import lax
        HEADS = 8
        DIM_HEAD = 64
        EPS = 1e-12

        def _l2norm(t):
            n = jnp.sqrt(jnp.sum(t * t, axis=-1, keepdims=True))
            return t / jnp.maximum(n, EPS)
        b, c, h, w = x_in.shape
        n = h * w
        x = x_in.transpose(0, 2, 3, 1).reshape(b, n, c)

        def proj(W):
            t = (x @ W).reshape(b, n, HEADS, DIM_HEAD)
            return t.transpose(0, 2, 3, 1)
        q = _l2norm(proj(Wq))
        k = _l2norm(proj(Wk))
        v = proj(Wv)
        attn = jnp.einsum('bhdn,bhen->bhde', k, q) * rescale
        attn = jax.nn.softmax(attn, axis=-1)
        out = jnp.einsum('bhde,bhen->bhdn', attn, v)
        out = out.transpose(0, 3, 1, 2).reshape(b, n, HEADS * DIM_HEAD)
        out_c = (out @ Wp + bp).reshape(b, h, w, c).transpose(0, 3, 1, 2)
        out_p = lax.conv_general_dilated(x_in, pos_k, window_strides=(1, 1), padding='SAME', dimension_numbers=('NCHW', 'OIHW', 'NCHW'), feature_group_count=c)
        return out_c + out_p

    def _gn(v, G=32, eps=1e-5):
        B_, C_, H_, W_ = v.shape
        g = v.reshape(B_, G, C_ // G, H_, W_)
        m = jnp.mean(g, axis=(2, 3, 4), keepdims=True)
        s = jnp.var(g, axis=(2, 3, 4), keepdims=True)
        return ((g - m) / jnp.sqrt(s + eps)).reshape(v.shape)

    def _ln_c(v, eps=1e-6):
        m = jnp.mean(v, axis=1, keepdims=True)
        s = jnp.var(v, axis=1, keepdims=True)
        return (v - m) / jnp.sqrt(s + eps)

    def _ln_t(v, eps=1e-5):
        m = jnp.mean(v, axis=-1, keepdims=True)
        s = jnp.var(v, axis=-1, keepdims=True)
        return (v - m) / jnp.sqrt(s + eps)

    def _to_tokens(v):
        B_, C_, H_, W_ = v.shape
        return v.reshape(B_, C_, H_ * W_).transpose(0, 2, 1)
    def _from_tokens(t, like):
        B_, C_, H_, W_ = like.shape
        return t.transpose(0, 2, 1).reshape(B_, C_, H_, W_)

    x = x + _L0_conv_ref(_gn(x), L0_conv_Wq, L0_conv_Wk, L0_conv_Wv, L0_conv_rescale, L0_conv_Wp, L0_conv_bp, L0_conv_pos_k)
    return x


_drawn_inputs = setup_inputs


def setup_inputs(seed=0):
    import zlib

    import numpy as np

    out = dict(_drawn_inputs(seed))
    spreads = {'L0_conv_rescale': (1.0, 0.6), 'L0_conv_bp': (0.0, 0.1)}
    factors = {'L0_conv_Wq': 8.0, 'L0_conv_Wk': 8.0, 'L0_conv_Wv': 7.007, 'L0_conv_Wp': 6.934}
    for name, (base, spread) in spreads.items():
        noise = np.random.default_rng([zlib.crc32(name.encode()), seed]).standard_normal(out[name].shape)
        drawn = base * np.exp(spread * noise) if base else spread * noise
        out[name] = jnp.asarray(drawn.astype(out[name].dtype))
    for name, factor in factors.items():
        out[name] = (out[name] * factor).astype(out[name].dtype)
    return out
```

```python
import numpy as np

import concourse.bass as bass
from concourse import mybir
from contextlib import ExitStack

F32 = mybir.dt.float32
ALU = mybir.AluOpType
ACT = mybir.ActivationFunctionType
AX = mybir.AxisListType

B, C, H, W = 2, 64, 256, 256
HEADS, DH = 8, 64
P = 2 * C
HALF = H // 2
PIX = H * W
GROUP = 2
NORM_EPS = 1e-5
LEAST_SQUARE = 1e-24

CHUNK = 16
CHUNKS = HALF // CHUNK
SLOT = CHUNK + 2
SLOTS = CHUNKS + 1
PIECE = 4
PIECES = CHUNK // PIECE
GROUPS = CHUNK // 2
GPP = GROUPS // PIECES
PAIRS = CHUNKS // 2
LAG = 2

CENTRE, TOP, BOTTOM = (0, 0), (-1, 0), (1, 0)
PE_SIDES = [(0, -1), (0, 1)]
DVE_SIDES = [(-1, -1), (-1, 1), (1, -1)]
POOL_SIDE = (1, 1)


def tap(dy, dx):
    return 3 * (dy + 1) + dx + 1


def span(d):
    return slice(max(0, -d), W - max(0, d)), slice(max(0, d), W + min(0, d))


def wait_from(eng, sem, value):
    if isinstance(value, int) and value <= 0:
        return
    eng.wait_ge(sem, value)


def build(nc, x, wq, wk, wv, rescale, wp, bp, pos_k, consts, out):
    ctx = ExitStack()
    with ctx:
        def sb(name, shape):
            return ctx.enter_context(nc.sbuf_tensor(name, shape, F32))

        def pb(name, shape):
            return ctx.enter_context(nc.psum_tensor(name, shape, F32))

        def sem(name):
            return ctx.enter_context(nc.semaphore(name))

        rows = sb("rows", [P, SLOTS * SLOT, W])
        stage = sb("stage", [P, 4, 512])
        xt = sb("xt", [P, 2, 4, 130])
        acc_out = sb("acc_out", [P, 2, PIECE, W])
        prod = sb("prod", [P, 2, PIECE, W])
        side = sb("side", [P, PIECE, W])
        const = sb("const", [P, 3 * P])
        ones = sb("ones", [C, C])
        w_mix = sb("w_mix", [P, P])
        w_side = sb("w_side", [P, 2, P])
        wqk = sb("wqk", [C, 2, HEADS * DH])
        wv_t = sb("wv_t", [DH, HEADS, C])
        wp_sb = sb("wp_sb", [DH, HEADS, C])
        taps = sb("taps", [P, 9])
        bp_sb = sb("bp_sb", [P, 1])
        resc = sb("resc", [DH, HEADS])
        taps_a = sb("taps_a", [P, B, 9])
        bias = sb("bias", [P, B])
        neg_mean = sb("neg_mean", [P, B])
        stacked = sb("stacked", [P, C + 1])
        gram_sb = sb("gram_sb", [P, C + 1])
        diag3 = sb("diag3", [C, 3, C])
        normed = sb("normed", [C, C])
        st = sb("st", [P, 16])
        zeros = sb("zeros", [P, P + 1])
        rk = sb("rk", [DH, HEADS])
        mx = sb("mx", [DH, HEADS])

        eye = const[:, 0:P]
        both = const[:, P:2 * P]
        pair = const[0:C, 2 * P:3 * P]
        eye64 = both[0:C, 0:C]
        prod_q, prod_k = stage[0:C, 0, :], stage[0:C, 1, :]
        proj_q = stage[0:C, 2, :]
        att = stage[0:C, 3, :].rearrange("d (h e) -> d h e", h=HEADS)
        rq = stage[0:C, 0, :]
        headed = stage[0:C, 0, :].rearrange("e (h c) -> e h c", h=HEADS)
        wv_raw = acc_out[0:C, 0, 0:2, :].rearrange("c r w -> c (r w)")
        mean, ex2, msq, var, dev, inv, tmp, scale, excess, neg_scale, centre1 = (st[:, j:j + 1] for j in range(2, 13))
        sums = st[:, 0:1]

        conv = pb("conv", [P, 2, PIECE, W])
        trans = pb("trans", [P, 2, 512])
        gram = pb("gram", [P, 512])
        misc = pb("misc", [P, 512])

        small_loaded = sem("small_loaded")
        loaded = [sem("loaded_even"), sem("loaded_odd")]
        stored = [sem("stored_even"), sem("stored_odd")]
        ones_ready = sem("ones_ready")
        wv_transposed = sem("wv_transposed")
        wv_copied = sem("wv_copied")
        staged = sem("staged")
        transposed = sem("transposed")
        xt_ready = sem("xt_ready")
        grammed = sem("grammed")
        gram_complete = sem("gram_complete")
        halves_stacked = sem("halves_stacked")
        halves_added = sem("halves_added")
        diag_ready = sem("diag_ready")
        group_sums = sem("group_sums")
        variance_ready = sem("variance_ready")
        deviation_ready = sem("deviation_ready")
        diagonals_ready = sem("diagonals_ready")
        rows_ready = sem("rows_ready")
        gram_normed = sem("gram_normed")
        projected = sem("projected")
        norm_terms = sem("norm_terms")
        norms_ready = sem("norms_ready")
        logits_ready = sem("logits_ready")
        norms_clamped = sem("norms_clamped")
        norms_rooted = sem("norms_rooted")
        logits_shifted = sem("logits_shifted")
        exps_ready = sem("exps_ready")
        att_ready = sem("att_ready")
        headed_ready = sem("headed_ready")
        headed_copied = sem("headed_copied")
        mixing_ready = sem("mixing_ready")
        weights_ready = sem("weights_ready")
        small_step = sem("small_step")
        centred = sem("centred")
        conv_ready = sem("conv_ready")
        tap_added = sem("tap_added")
        acc_ready = sem("acc_ready")
        prod_ready = sem("prod_ready")
        side_ready = sem("side_ready")
        side_added = sem("side_added")
        summed = sem("summed")

        block = ctx.enter_context(nc.Block())

        def pieces(b, i):
            for e in range(2):
                for p in range(PIECES):
                    chunk = 2 * i + e
                    first = (chunk + 1 - b) * SLOT + 1 + PIECE * p
                    yield b * CHUNKS * PIECES + PIECES * chunk + p, first, e, p

        def gram_groups(b, i, e, p, lag):
            place = PIECES * e + p - lag
            if isinstance(i, int) and i == 0 and place < 0:
                return
            for g in range(GPP * place, GPP * (place + 1)):
                chunk, inner = g // GROUPS, g % GROUPS
                number = b * CHUNKS * GROUPS + 2 * GROUPS * i + g
                yield number, (2 * i + chunk + 1 - b) * SLOT + 1 + 2 * inner, g

        def flat(first, n):
            return rows[:, bass.ds(first, n), :]

        @block.sync
        def _(sp):
            xs = x.rearrange("b c (s h) w -> b s c h w", s=2)
            ys = out.rearrange("b c (s h) w -> b s c h w", s=2)

            def load(b, k, before, place=None):
                s = loaded[k % 2] if place is None else loaded[place]
                wait_from(sp, s, before)
                inner = not isinstance(k, int) or 0 < k < CHUNKS - 1
                for half in range(2):
                    dst0, n = (k + 1 - b) * SLOT, SLOT
                    src0 = HALF * half + CHUNK * k - 1
                    if not inner and k == 0 and half == 0:
                        dst0, src0, n = dst0 + 1, src0 + 1, SLOT - 1
                    if not inner and k == CHUNKS - 1 and half == 1:
                        n = SLOT - 1
                    sp.dma_start(rows[C * half:C * (half + 1), bass.ds(dst0, n), :],
                                 x[b, :, bass.ds(src0, n), :]).then_inc(s, 16)

            def store(b, i, e):
                for number, _, e2, p in pieces(b, i):
                    if e2 != e:
                        continue
                    k = 2 * i + e
                    sp.wait_ge(summed, number + 1)
                    for half in range(2):
                        sp.dma_start(out[b, :, bass.ds(HALF * half + CHUNK * k + PIECE * p, PIECE), :],
                                     acc_out[C * half:C * (half + 1), p % 2, :, :]).then_inc(stored[p % 2], 16)

            sp.dma_start(const[:, :], consts).then_inc(small_loaded, 16)
            load(0, 0, 0)
            load(0, 1, 0)
            sp.dma_start(wv_raw, wv).then_inc(small_loaded, 16)
            sp.dma_start(wqk[:, 0, :], wq).then_inc(small_loaded, 16)
            sp.dma_start(wqk[:, 1, :], wk).then_inc(small_loaded, 16)
            sp.dma_start(wp_sb[:, :, :], wp.rearrange("(h d) c -> d h c", h=HEADS)).then_inc(small_loaded, 16)
            sp.dma_start(resc[:, :], rescale.rearrange("h a b -> (a b) h").broadcast_to([DH, HEADS]))\
                .then_inc(small_loaded, 16)
            for half in range(2):
                at = slice(C * half, C * (half + 1))
                sp.dma_start(taps[at, :], pos_k.rearrange("c a i j -> c (a i j)")).then_inc(small_loaded, 16)
                sp.dma_start(bp_sb[at, :], bp.rearrange("(c a) -> c a", a=1)).then_inc(small_loaded, 16)
            for k in range(2, CHUNKS):
                load(0, k, 32 * (k // 2))
            load(1, 0, 32 * PAIRS)

            def first_image(i):
                for e in range(2):
                    store(0, i, e)
                    if not (isinstance(i, int) and 2 * i + e == CHUNKS - 1):
                        k = 2 * i + e + 1
                        load(1, k, 32 * (PAIRS + (i + e)), place=(e + 1) % 2)

            with sp.Fori(0, PAIRS - 1) as i:
                first_image(i)
            first_image(PAIRS - 1)
            with sp.Fori(0, PAIRS) as i:
                for e in range(2):
                    store(1, i, e)
            for s in stored:
                sp.wait_ge(s, 32 * B * CHUNKS * PIECES // 2)

        @block.tensor
        def _(pe):
            def transpose_group(number, g):
                pe.wait_ge(staged, number + 1)
                wait_from(pe, xt_ready, number - 1)
                for j in range(4):
                    last = nc.tensor.transpose(trans[:, g % 2, P * j:P * (j + 1)], stage[:, g % 4, P * j:P * (j + 1)],
                                               eye)
                last.then_inc(transposed, 1)

            def multiply_group(number, g):
                pe.wait_ge(xt_ready, number + 1)
                for j in range(4):
                    last = nc.tensor.matmul(gram[:, 0:P + 1], xt[:, g % 2, j, 0:P], xt[:, g % 2, j, 0:P + 1],
                                            start=False, stop=False, skip_group_check=True)
                last.then_inc(grammed, 1)

            def open_gram():
                nc.tensor.matmul(gram[:, 0:P + 1], zeros[:, 0:P], zeros[:, :], start=True, stop=False, skip_group_check=True)

            def close_gram():
                nc.tensor.matmul(gram[:, 0:P + 1], zeros[:, 0:P], zeros[:, :], start=False, stop=True,
                                 skip_group_check=True).then_inc(gram_complete, 1)

            def gram_step(groups, carried):
                for number, _, g in groups:
                    transpose_group(number, g)
                    if not (isinstance(number, int) and number == carried):
                        multiply_group(number - 1, g - 1)

            def main(b, i, with_gram):
                for number, first, e, p in pieces(b, i):
                    if p == 0:
                        pe.wait_ge(centred, b * CHUNKS + 2 * i + e + 1)
                    wait_from(pe, acc_ready, number - 1)
                    for dy, dx in [CENTRE] + PE_SIDES:
                        o, n = span(dx)
                        w = w_mix[:, :] if (dy, dx) == CENTRE else w_side[:, PE_SIDES.index((dy, dx)), :]
                        for two in range(0, PIECE, 2):
                            last = nc.tensor.matmul(conv[:, p % 2, two:two + 2, o], w,
                                                    rows[:, bass.ds(first + two + dy, 2), n],
                                                    start=(dy, dx) == CENTRE, stop=(dy, dx) == PE_SIDES[-1],
                                                    skip_group_check=True)
                    last.then_inc(conv_ready, 1)
                    if with_gram:
                        gram_step(gram_groups(1, i, e, p, LAG), CHUNKS * GROUPS)

            def softmax_part(b):
                n = b + 1
                pe.wait_ge(halves_stacked, n)
                nc.tensor.matmul(misc[:, 0:C + 1], both, stacked[:, :], start=True, stop=True).then_inc(halves_added, 1)
                pe.wait_ge(diag_ready, n)
                nc.tensor.matmul(misc[:, P:P + 2], pair, st[0:C, 0:2], start=True, stop=True).then_inc(group_sums, 1)
                pe.wait_ge(diagonals_ready, n)
                nc.tensor.matmul(misc[0:C, 0:3 * C], ones[:, :], diag3[:, :, :].rearrange("k a c -> k (a c)"),
                                 start=True, stop=True).then_inc(rows_ready, 1)
                pe.wait_ge(gram_normed, n)
                nc.tensor.matmul(trans[0:C, 0, :], normed[:, :], wqk[:, 0, :], start=True, stop=True)
                nc.tensor.matmul(trans[0:C, 1, :], normed[:, :], wqk[:, 1, :], start=True, stop=True)\
                    .then_inc(projected, 1)
                pe.wait_ge(norm_terms, n)
                nc.tensor.matmul(misc[0:C, :], ones[:, :], prod_q, start=True, stop=True)
                for h in range(HEADS):
                    at = slice(h * DH, (h + 1) * DH)
                    last = nc.tensor.matmul(gram[0:DH, h:h + 1], prod_k[:, at], ones[:, 0:1], start=True, stop=True)
                last.then_inc(norms_ready, 1)
                for h in range(HEADS):
                    at = slice(h * DH, (h + 1) * DH)
                    last = nc.tensor.matmul(trans[0:DH, 0, at], wqk[:, 1, at], proj_q[:, at], start=True, stop=True)
                last.then_inc(logits_ready, 1)
                pe.wait_ge(att_ready, n)
                for h in range(HEADS):
                    at = slice(h * DH, (h + 1) * DH)
                    last = nc.tensor.matmul(trans[0:DH, 1, at], att[:, h, :], wp_sb[:, h, :], start=True, stop=True)
                last.then_inc(headed_ready, 1)
                pe.wait_ge(headed_copied, n)
                for half in range(2):
                    for h in range(HEADS):
                        last = nc.tensor.matmul(misc[C * half:C * (half + 1), 0:C], wv_t[:, h, :], headed[:, h, :],
                                                start=h == 0, stop=h == HEADS - 1)
                last.then_inc(mixing_ready, 1)

            pe.wait_ge(small_loaded, 16 * 10)
            for h in range(HEADS):
                last = nc.tensor.transpose(trans[0:DH, 0, C * h:C * (h + 1)], wv_raw[:, DH * h:DH * (h + 1)], eye64)
            last.then_inc(wv_transposed, 1)
            pe.wait_ge(ones_ready, 1)
            pe.wait_ge(wv_copied, 1)

            def gram_pass(i):
                for e in range(2):
                    for p in range(PIECES):
                        gram_step(gram_groups(0, i, e, p, 0), 0)

            open_gram()
            gram_pass(0)
            with pe.Fori(1, PAIRS) as i:
                gram_pass(i)
            multiply_group(CHUNKS * GROUPS - 1, GROUPS - 1)
            close_gram()
            softmax_part(0)
            pe.wait_ge(weights_ready, 1)
            open_gram()
            main(0, 0, True)
            with pe.Fori(1, PAIRS) as i:
                main(0, i, True)
            for number, _, g in list(gram_groups(1, PAIRS, 0, 0, LAG)) + list(gram_groups(1, PAIRS, 0, 1, LAG)):
                transpose_group(number, g)
                multiply_group(number - 1, g - 1)
            multiply_group(B * CHUNKS * GROUPS - 1, GROUPS - 1)
            close_gram()
            softmax_part(1)
            pe.wait_ge(weights_ready, 2)
            with pe.Fori(0, PAIRS) as i:
                main(1, i, False)

        @block.scalar
        def _(act):
            def copy_out(number, g):
                act.wait_ge(transposed, number + 1)
                wait_from(act, grammed, number - 1)
                nc.scalar.copy(xt[:, g % 2, :, 0:P], trans[:, g % 2, :].rearrange("p (j n) -> p j n", j=4))\
                    .then_inc(xt_ready, 1)

            def centre(b, chunk):
                v = flat((chunk + 1 - b) * SLOT, SLOT)
                act.wait_ge(weights_ready, b + 1)
                nc.scalar.activation(v, v, ACT.Identity, bias=neg_mean[:, b:b + 1]).then_inc(centred, 1)

            def main(b, i, with_gram, last_pair):
                for number, first, e, p in pieces(b, i):
                    if p == 0:
                        act.wait_ge(centred, b * CHUNKS + 2 * i + e + 1)
                        if not (last_pair and e == 1):
                            centre(b, 2 * i + e + 1)
                    wait_from(act, summed, number - 1)
                    wait_from(act, side_added, number)
                    nc.scalar.activation(prod[:, p % 2, :, :], flat(first + BOTTOM[0], PIECE), ACT.Identity,
                                         bias=bias[:, b:b + 1], scale=taps_a[:, b, tap(*BOTTOM):tap(*BOTTOM) + 1])\
                        .then_inc(prod_ready, 1)
                    nc.scalar.activation(side[:, :, :], flat(first + POOL_SIDE[0], PIECE), ACT.Identity,
                                         scale=taps_a[:, b, tap(*POOL_SIDE):tap(*POOL_SIDE) + 1])\
                        .then_inc(side_ready, 1)
                    if with_gram:
                        for n, _, g in gram_groups(1, i, e, p, LAG):
                            copy_out(n, g)

            def softmax_part(b):
                n = b + 1
                act.wait_ge(variance_ready, n)
                nc.scalar.activation(dev, var, ACT.Sqrt).then_inc(deviation_ready, 1)
                act.wait_ge(norms_clamped, n)
                nc.scalar.activation(rq[:, :], rq[:, :], ACT.Sqrt)
                nc.scalar.activation(rk[:, :], rk[:, :], ACT.Sqrt).then_inc(norms_rooted, 1)
                act.wait_ge(logits_shifted, n)
                nc.scalar.activation(att, att, ACT.Exp).then_inc(exps_ready, 1)
                centre(b, 0)

            def gram_pass(i):
                for e in range(2):
                    for p in range(PIECES):
                        for n, _, g in gram_groups(0, i, e, p, 0):
                            copy_out(n, g)

            act.wait_ge(ones_ready, 1)
            gram_pass(0)
            with act.Fori(1, PAIRS) as i:
                gram_pass(i)
            softmax_part(0)
            main(0, 0, True, False)
            with act.Fori(1, PAIRS - 1) as i:
                main(0, i, True, False)
            main(0, PAIRS - 1, True, True)
            for n, _, g in list(gram_groups(1, PAIRS, 0, 0, LAG)) + list(gram_groups(1, PAIRS, 0, 1, LAG)):
                copy_out(n, g)
            softmax_part(1)
            with act.Fori(0, PAIRS - 1) as i:
                main(1, i, False, False)
            main(1, PAIRS - 1, False, True)

        @block.vector
        def _(dve):
            steps = [0]

            def then(instruction):
                steps[0] += 1
                instruction.then_inc(small_step, 1)
                dve.wait_ge(small_step, steps[0])

            def stage_group(b, i, number, first, g):
                if g % GROUPS == 0:
                    chunk = g // GROUPS
                    dve.wait_ge(loaded[chunk % 2], 32 * (b * PAIRS + i + 1) if chunk >= 0 else 32 * (b * PAIRS + i))
                wait_from(dve, transposed, number - 3)
                nc.vector.tensor_copy(stage[:, g % 4, :], flat(first, 2).rearrange("p r w -> p (r w)"))\
                    .then_inc(staged, 1)

            def main(b, i, with_gram):
                for number, first, e, p in pieces(b, i):
                    if with_gram:
                        for n, f, g in gram_groups(1, i, e, p, LAG):
                            stage_group(1, i, n, f, g)
                    if p == 0:
                        dve.wait_ge(centred, b * CHUNKS + 2 * i + e + 1)
                    dve.wait_ge(conv_ready, number + 1)
                    for j, (dy, dx) in enumerate(DVE_SIDES):
                        o, n = span(dx)
                        v = conv[:, p % 2, :, o]
                        if j:
                            dve.wait_ge(tap_added, len(DVE_SIDES) * number + j)
                        nc.vector.scalar_tensor_tensor(out=v, in0=rows[:, bass.ds(first + dy, PIECE), n],
                                                       scalar=taps_a[:, b, tap(dy, dx):tap(dy, dx) + 1], in1=v,
                                                       op0=ALU.mult, op1=ALU.add).then_inc(tap_added, 1)
                    dve.wait_ge(tap_added, len(DVE_SIDES) * (number + 1))
                    wait_from(dve, stored[p % 2], 32 * ((number - p) // 2 + p // 2) if isinstance(number, int) else
                              number_times(b, i, e, p))
                    nc.vector.scalar_tensor_tensor(out=acc_out[:, p % 2, :, :].rearrange("p r w -> p (r w)"),
                                                   in0=flat(first + TOP[0], PIECE).rearrange("p r w -> p (r w)"),
                                                   scalar=taps_a[:, b, tap(*TOP):tap(*TOP) + 1],
                                                   in1=conv[:, p % 2, :, :].rearrange("p r w -> p (r w)"),
                                                   op0=ALU.mult, op1=ALU.add).then_inc(acc_ready, 1)

            def number_times(b, i, e, p):
                return 32 * (b * CHUNKS * PIECES // 2 + PIECES * i + (PIECES * e + p) // 2)

            def softmax_part(b):
                n = b + 1
                wide = lambda v: v.unsqueeze(2).broadcast_to([DH, HEADS, DH])
                dve.wait_ge(gram_complete, n)
                nc.vector.tensor_copy(stacked[0:C, 0:C], gram[0:C, 0:C])
                nc.vector.tensor_copy(stacked[C:P, 0:C], gram[C:P, C:P])
                nc.vector.tensor_copy(stacked[:, C:C + 1], gram[:, P:P + 1]).then_inc(halves_stacked, 1)
                dve.wait_ge(halves_added, n)
                then(nc.vector.tensor_copy(gram_sb[:, :], misc[:, 0:C + 1]))
                then(nc.vector.tensor_tensor(stacked[:, 0:C], gram_sb[:, 0:C], both[:, 0:C], ALU.mult))
                nc.vector.tensor_copy(sums, gram_sb[:, C:C + 1])
                nc.vector.reduce_sum(st[:, 1:2], stacked[:, 0:C], AX.X).then_inc(diag_ready, 1)
                dve.wait_ge(group_sums, n)
                then(nc.vector.tensor_scalar(st[:, 2:4], misc[:, P:P + 2], 1.0 / (GROUP * PIX), None, ALU.mult))
                then(nc.vector.tensor_tensor(msq, mean, mean, ALU.mult))
                then(nc.vector.tensor_tensor(var, ex2, msq, ALU.subtract))
                steps[0] += 0
                nc.vector.tensor_scalar(var, var, 0.0, NORM_EPS, ALU.max, ALU.add).then_inc(variance_ready, 1)
                nc.vector.tensor_scalar(neg_mean[:, b:b + 1], mean, -1.0, None, ALU.mult)
                then(nc.vector.tensor_tensor(bias[:, b:b + 1], mean, bp_sb[:, :], ALU.add))
                then(nc.vector.scalar_tensor_tensor(out=excess, in0=neg_mean[:, b:b + 1], scalar=float(PIX), in1=sums,
                                                    op0=ALU.mult, op1=ALU.add))
                dve.wait_ge(deviation_ready, n)
                dve.wait_ge(variance_ready, n)
                then(nc.vector.reciprocal(inv, dev))
                then(nc.vector.tensor_tensor(tmp, inv, inv, ALU.mult))
                then(nc.vector.tensor_tensor(tmp, tmp, var, ALU.mult))
                then(nc.vector.tensor_scalar(tmp, tmp, -0.5, 1.5, ALU.mult, ALU.add))
                then(nc.vector.tensor_tensor(scale, inv, tmp, ALU.mult))
                nc.vector.tensor_scalar(neg_scale, scale, -1.0, None, ALU.mult)
                for j, v in enumerate((mean, excess, scale)):
                    last = nc.vector.tensor_scalar(diag3[:, j, :], eye64, v[0:C, :], None, ALU.mult)
                last.then_inc(diagonals_ready, 1)
                then(nc.vector.tensor_scalar(taps_a[:, b, :], taps[:, :], scale, None, ALU.mult))
                dve.wait_ge(rows_ready, n)
                then(nc.vector.scalar_tensor_tensor(out=normed[:, :], in0=misc[0:C, 0:C], scalar=st[0:C, 0:1],
                                                    in1=gram_sb[0:C, 0:C], op0=ALU.mult, op1=ALU.subtract))
                then(nc.vector.scalar_tensor_tensor(out=normed[:, :], in0=misc[0:C, C:2 * C], scalar=mean[0:C, :],
                                                    in1=normed[:, :], op0=ALU.mult, op1=ALU.add))
                nc.vector.scalar_tensor_tensor(out=normed[:, :], in0=normed[:, :], scalar=neg_scale[0:C, :],
                                               in1=misc[0:C, 2 * C:3 * C], op0=ALU.mult, op1=ALU.mult)\
                    .then_inc(gram_normed, 1)
                dve.wait_ge(projected, n)
                nc.vector.tensor_tensor(prod_q, trans[0:C, 0, :], wqk[:, 0, :], ALU.mult)
                nc.vector.tensor_copy(proj_q, trans[0:C, 0, :])
                nc.vector.tensor_tensor(prod_k, trans[0:C, 1, :], wqk[:, 1, :], ALU.mult).then_inc(norm_terms, 1)
                dve.wait_ge(norms_ready, n)
                nc.vector.tensor_scalar(rq[:, :], misc[0:C, :], LEAST_SQUARE, None, ALU.max)
                nc.vector.tensor_scalar(rk[:, :], gram[0:DH, 0:HEADS], LEAST_SQUARE, None, ALU.max)\
                    .then_inc(norms_clamped, 1)
                dve.wait_ge(norms_rooted, n)
                then(nc.vector.reciprocal(rk[:, :], rk[:, :]))
                then(nc.vector.reciprocal(rq[:, :], rq[:, :]))
                then(nc.vector.tensor_tensor(rk[:, :], rk[:, :], resc[:, :], ALU.mult))
                dve.wait_ge(logits_ready, n)
                then(nc.vector.tensor_tensor(att, trans[0:C, 0, :].rearrange("d (h e) -> d h e", h=HEADS),
                                             rq[:, :].rearrange("d (h e) -> d h e", h=HEADS), ALU.mult))
                then(nc.vector.tensor_tensor(att, att, wide(rk[:, :]), ALU.mult))
                then(nc.vector.reduce_max(mx[:, :], att, AX.X))
                nc.vector.tensor_tensor(att, att, wide(mx[:, :]), ALU.subtract).then_inc(logits_shifted, 1)
                dve.wait_ge(exps_ready, n)
                then(nc.vector.reduce_sum(mx[:, :], att, AX.X))
                then(nc.vector.reciprocal(mx[:, :], mx[:, :]))
                nc.vector.tensor_tensor(att, att, wide(mx[:, :]), ALU.mult).then_inc(att_ready, 1)
                dve.wait_ge(headed_ready, n)
                nc.vector.tensor_copy(headed, trans[0:C, 1, :].rearrange("e (h c) -> e h c", h=HEADS))\
                    .then_inc(headed_copied, 1)
                then(nc.vector.tensor_scalar_add(centre1, taps_a[:, b, tap(*CENTRE):tap(*CENTRE) + 1], 1.0))
                dve.wait_ge(mixing_ready, n)
                for half in range(2):
                    at = slice(C * half, C * (half + 1))
                    nc.vector.tensor_scalar(w_mix[at, at], misc[at, 0:C], scale[at, :], None, ALU.mult)
                    edge = SLOT * (1 - b) if half == 0 else SLOT * (CHUNKS + 1 - b) - 1
                    nc.vector.tensor_scalar(rows[at, edge, :], const[at, 0:W], 0.0, mean[at, :], ALU.mult, ALU.add)
                for j, (dy, dx) in enumerate(PE_SIDES):
                    t = tap(dy, dx)
                    last = nc.vector.tensor_scalar(w_side[:, j, :], eye, taps_a[:, b, t:t + 1], None, ALU.mult)
                then(last)
                nc.vector.scalar_tensor_tensor(out=w_mix[:, :], in0=eye, scalar=centre1, in1=w_mix[:, :],
                                               op0=ALU.mult, op1=ALU.add).then_inc(weights_ready, 1)

            nc.vector.memset(w_mix[:, :], 0.0)
            nc.vector.memset(zeros[:, :], 0.0)
            nc.vector.memset(xt[:, :, :, P:P + 2], 1.0)
            nc.vector.memset(ones[:, :], 1.0).then_inc(ones_ready, 1)
            dve.wait_ge(wv_transposed, 1)
            nc.vector.tensor_copy(wv_t[:, :, :], trans[0:DH, 0, :].rearrange("e (h c) -> e h c", h=HEADS))\
                .then_inc(wv_copied, 1)

            def gram_pass(i):
                for e in range(2):
                    for p in range(PIECES):
                        for n, f, g in gram_groups(0, i, e, p, 0):
                            stage_group(0, i, n, f, g)

            gram_pass(0)
            with dve.Fori(1, PAIRS) as i:
                gram_pass(i)
            softmax_part(0)
            main(0, 0, True)
            with dve.Fori(1, PAIRS) as i:
                main(0, i, True)
            for n, f, g in list(gram_groups(1, PAIRS, 0, 0, LAG)) + list(gram_groups(1, PAIRS, 0, 1, LAG)):
                stage_group(1, PAIRS, n, f, g)
            softmax_part(1)
            with dve.Fori(0, PAIRS) as i:
                main(1, i, False)

        @block.gpsimd
        def _(pool):
            def main(b, i):
                for number, first, e, p in pieces(b, i):
                    o, n = span(POOL_SIDE[1])
                    v = prod[:, p % 2, :, o]
                    pool.wait_ge(prod_ready, number + 1)
                    pool.wait_ge(side_ready, number + 1)
                    nc.gpsimd.tensor_tensor(v, v, side[:, :, n], ALU.add).then_inc(side_added, 1)
                    pool.wait_ge(acc_ready, number + 1)
                    pool.wait_ge(side_added, number + 1)
                    nc.gpsimd.tensor_tensor(acc_out[:, p % 2, :, :], acc_out[:, p % 2, :, :], prod[:, p % 2, :, :],
                                            ALU.add).then_inc(summed, 1)

            for b in range(B):
                with pool.Fori(0, PAIRS) as i:
                    main(b, i)


_INS = ["x", "L0_conv_Wq", "L0_conv_Wk", "L0_conv_Wv", "L0_conv_rescale", "L0_conv_Wp", "L0_conv_bp", "L0_conv_pos_k"]


def _constants():
    n = np.arange(P)
    eye = n[:, None] == n[None, :]
    both = n[:, None] % C == n[None, :] % C
    pair = (n[:, None] % C) // GROUP == (n[None, :] % C) // GROUP
    return np.concatenate([eye, both, pair], axis=1).astype(np.float32)


def kernel(**inputs):
    import concourse.bacc as _bacc
    from concourse.bass_utils import run_bass_kernel_spmd as _run

    nc = _bacc.Bacc("TRN2", target_bir_lowering=False, num_devices=1)
    arrays, args = {}, []
    for name, a in [(n, inputs[n]) for n in _INS] + [("constants", _constants())]:
        a = np.ascontiguousarray(a)
        arrays[f"in_{name}"] = a
        args.append(nc.dram_tensor(f"in_{name}", a.shape, mybir.dt.from_np(a.dtype), kind="ExternalInput").ap())
    args.append(nc.dram_tensor("out_0", (B, C, H, W), F32, kind="ExternalOutput").ap())
    build(nc, *args)
    r = _run(nc, [arrays], core_ids=[0])
    return r.results[0]["out_0"]
```

```python
import numpy as np

import concourse.bass as bass
from concourse import mybir
from contextlib import ExitStack

F32 = mybir.dt.float32
ALU = mybir.AluOpType
ACT = mybir.ActivationFunctionType
AX = mybir.AxisListType

B, C, H, W = 2, 64, 256, 256
HEADS, DH = 8, 64
P = 2 * C
HALF = H // 2
PIX = H * W
GROUP = 2
NORM_EPS = 1e-5
LEAST_SQUARE = 1e-24

CHUNK = 16
CHUNKS = HALF // CHUNK
PIECE = 4
PIECES = CHUNK // PIECE
STRIP = 2
STRIPS = PIECE // STRIP
STORE_INCS = 16
PAIRS = CHUNKS // 2
IMAGE_PIECES = CHUNKS * PIECES
GROUPS = CHUNK // 2
BLOCKS = 2 * W // P
FIRST_ROWS = 4

HEAD_CHUNKS = 2
HEAD_ROWS = HEAD_CHUNKS * CHUNK + 2
ROWS = HEAD_ROWS + HALF + 2

GPP = 2
HEAD_FIRST = CHUNKS * GROUPS
DIRECT_FIRST = HEAD_FIRST + HEAD_CHUNKS * GROUPS
DIRECT_CHUNKS = (6, 7)
COPIED_FIRST = DIRECT_FIRST + len(DIRECT_CHUNKS) * GROUPS
ALL_GROUPS = 2 * CHUNKS * GROUPS
GRAM_PIECES = (ALL_GROUPS - DIRECT_FIRST) // GPP

CENTRE, TOP, BOTTOM = (0, 0), (-1, 0), (1, 0)
SIDES = [(0, -1), (0, 1), (-1, -1), (-1, 1), (1, -1), (1, 1)]
POOL_SIDE = SIDES[5]


def pe_sides(with_gram, p):
    return SIDES[:1] if with_gram and p % 2 else SIDES[:2]


def dve_sides(with_gram, p):
    return [t for t in SIDES[:5] if t not in pe_sides(with_gram, p)]


def place(b, chunk):
    if b == 0:
        return HEAD_ROWS + 1
    if isinstance(chunk, int) and chunk < HEAD_CHUNKS:
        return 1
    return HEAD_ROWS - (HEAD_CHUNKS * CHUNK - 1)


def fresh(b, chunk):
    if isinstance(chunk, int) and (chunk == 0 or (b == 1 and chunk == HEAD_CHUNKS)):
        return CHUNK * chunk - 1, CHUNK + 2
    return CHUNK * chunk + 1, CHUNK


QUARTERS = [(0,), (1,), (2, 3), ()]
FILL = (4, 2, 3, 3, 4)
DVE_STEPS = {0: ["stack"], 1: ["diagonal"], 2: ["moments"], 3: ["scales"], 4: ["gram"], 5: ["terms"],
             6: ["clamp", "invert"], 7: ["shift", "divide", "headed", "weights"]}
PE_STEPS = {1: ["halves"], 2: ["groups"], 4: ["rows"], 5: ["project"], 6: ["logits"],
            7: ["queries", "values", "mix"]}
ACT_STEPS = {2: ["deviation"], 4: ["centre"], 6: ["norms"], 7: ["exp"]}


def tap(dy, dx):
    return 3 * (dy + 1) + dx + 1


def strip(s):
    return slice(STRIP * s, STRIP * (s + 1))


def span(d):
    return slice(max(0, -d), W - max(0, d)), slice(max(0, d), W + min(0, d))


def wait_from(eng, sem, value):
    if isinstance(value, int) and value <= 0:
        return
    eng.wait_ge(sem, value)


def build(nc, x, wq, wk, wv, rescale, wp, bp, pos_k, consts, out):
    ctx = ExitStack()
    with ctx:
        def sb(name, shape):
            return ctx.enter_context(nc.sbuf_tensor(name, shape, F32))

        def pb(name, shape):
            return ctx.enter_context(nc.psum_tensor(name, shape, F32))

        def sem(name):
            return ctx.enter_context(nc.semaphore(name))

        rows = sb("rows", [P, ROWS, W])
        stage = sb("stage", [P, 4, 512])
        xt = sb("xt", [P, 2, BLOCKS, P + 2])
        acc_out = sb("acc_out", [P, 2, PIECE, W])
        prod = sb("prod", [P, 2, PIECE, W])
        side = sb("side", [P, PIECE, W])
        const = sb("const", [P, 3 * P])
        ones = sb("ones", [C, C])
        w_mix = sb("w_mix", [P, P])
        w_side = sb("w_side", [P, 2, P])
        wqk = sb("wqk", [C, 2, HEADS * DH])
        wv_t = sb("wv_t", [DH, HEADS, C])
        wp_sb = sb("wp_sb", [DH, HEADS, C])
        taps = sb("taps", [P, 9])
        bp_sb = sb("bp_sb", [P, 1])
        resc = sb("resc", [DH, HEADS])
        taps_a = sb("taps_a", [P, B, 9])
        bias = sb("bias", [P, B])
        neg_mean = sb("neg_mean", [P, B])
        st = sb("st", [P, 16])
        roots = sb("roots", [DH, 2, HEADS])
        mx = sb("mx", [DH, HEADS])
        tiny = sb("tiny", [P, 2])

        eye = const[:, 0:P]
        both = const[:, P:2 * P]
        pair = const[0:C, 2 * P:3 * P]
        eye64 = both[0:C, 0:C]
        wv_raw = acc_out[0:C, 0, 0:2, :].rearrange("c r w -> c (r w)")
        mean, ex2, msq, var, dev, inv, tmp, scale, excess, neg_scale, centre1 = (st[:, j:j + 1] for j in range(2, 13))
        sums = st[:, 0:1]

        conv = pb("conv", [P, 2, PIECE, W])
        trans = pb("trans", [P, 2, 512])
        gram = pb("gram", [P, 512])
        misc = pb("misc", [P, 512])

        conv_banks = conv[:, :, :, :].rearrange("p n r w -> p (n r w)").rearrange("p (k c) -> p k c", k=4)
        prod_rows = prod[:, :, :, :].rearrange("p n r w -> p (n r w)").rearrange("p (k c) -> p k c", k=4)
        BANKS = [[conv_banks[:, k, :] for k in range(4)], [trans[:, 0, :], trans[:, 1, :], gram[:, :], misc[:, :]]]
        early = [prod_rows[:, 2, :], stage[:, 2, :]]
        STACKED, GRAM = [v[:, 0:C + 1] for v in early], [v[:, P:P + C + 1] for v in early]
        NORMED = [v[0:C, 2 * P:2 * P + C] for v in early]
        ZERO_WEIGHTS = w_mix[0:C, C:P]
        SCRATCH = [[prod_rows[0:C, k, :] for k in range(4)], [stage[0:C, k, :] for k in range(4)]]

        const_loaded = sem("const_loaded")
        first_rows_loaded = sem("first_rows_loaded")
        small_loaded = sem("small_loaded")
        loaded = [sem("loaded_even"), sem("loaded_odd")]
        stored = [[sem("stored_even_0"), sem("stored_even_1")], [sem("stored_odd_0"), sem("stored_odd_1")]]
        ones_ready = sem("ones_ready")
        wv_transposed = sem("wv_transposed")
        wv_copied = sem("wv_copied")
        staged = [sem("staged_even"), sem("staged_odd")]
        transposed = sem("transposed")
        xt_ready = sem("xt_ready")
        grammed = sem("grammed")
        gram_complete = sem("gram_complete")
        halves_stacked = sem("halves_stacked")
        halves_added = sem("halves_added")
        diag_ready = sem("diag_ready")
        group_sums = sem("group_sums")
        variance_ready = sem("variance_ready")
        mean_ready = sem("mean_ready")
        deviation_ready = sem("deviation_ready")
        diagonals_ready = sem("diagonals_ready")
        rows_ready = sem("rows_ready")
        gram_normed = sem("gram_normed")
        projected = sem("projected")
        norm_terms = sem("norm_terms")
        norms_ready = sem("norms_ready")
        logits_ready = sem("logits_ready")
        norms_clamped = sem("norms_clamped")
        norms_rooted = sem("norms_rooted")
        query_diagonals = sem("query_diagonals")
        query_rows = sem("query_rows")
        logits_shifted = sem("logits_shifted")
        exps_ready = sem("exps_ready")
        att_ready = sem("att_ready")
        headed_ready = sem("headed_ready")
        headed_copied = sem("headed_copied")
        mixing_ready = sem("mixing_ready")
        weights_ready = sem("weights_ready")
        small_step = sem("small_step")
        centred = sem("centred")
        conv_ready = sem("conv_ready")
        tap_added = sem("tap_added")
        acc_ready = sem("acc_ready")
        prod_ready = sem("prod_ready")
        side_ready = sem("side_ready")
        side_added = sem("side_added")
        summed = sem("summed")

        block = ctx.enter_context(nc.Block())

        def pieces(b, i):
            for e in range(2):
                for p in range(PIECES):
                    chunk = 2 * i + e
                    yield b * IMAGE_PIECES + PIECES * chunk + p, place(b, chunk) + CHUNK * chunk + PIECE * p, e, p

        def flat(first, n):
            return rows[:, bass.ds(first, n), :]

        def has_gram(b, i):
            return b == 0 and not (isinstance(i, int) and i == PAIRS - 1)

        @block.sync
        def _(sp):
            def load(b, k, before, parity=None):
                s = loaded[k % 2 if parity is None else parity]
                wait_from(sp, s, before)
                row, n = fresh(b, k)
                edge = (isinstance(k, int) and k == 0, isinstance(k, int) and k == CHUNKS - 1)
                for half in range(2):
                    r0, m = row, n
                    if edge[0] and half == 0:
                        r0, m = r0 + 1, m - 1
                    if edge[1] and half == 1:
                        m -= 1
                    at = slice(C * half, C * (half + 1))
                    if b == 0 and edge[0]:
                        m0 = FIRST_ROWS - r0
                        sp.dma_start(rows[at, place(b, k) + r0:place(b, k) + r0 + m0, :],
                                     x[b, :, HALF * half + r0:HALF * half + r0 + m0, :]).then_inc(first_rows_loaded, 16)
                        r0, m = r0 + m0, m - m0
                    sp.dma_start(rows[at, bass.ds(place(b, k) + r0, m), :],
                                 x[b, :, bass.ds(HALF * half + r0, m), :]).then_inc(s, 16)

            def store(b, i, number, e, p):
                for s in range(STRIPS):
                    sp.wait_ge(summed, STRIPS * number + s + 1)
                    row = CHUNK * (2 * i + e) + PIECE * p + STRIP * s
                    sp.dma_start(out[b].rearrange("c (h r) w -> h c r w", h=2)[:, :, bass.ds(row, STRIP), :],
                                 acc_out[:, p % 2, strip(s), :]).then_inc(stored[p % 2][s], 16)

            def load_group(n):
                chunk = DIRECT_CHUNKS[(n - DIRECT_FIRST) // GROUPS]
                row = CHUNK * chunk + 2 * ((n - DIRECT_FIRST) % GROUPS)
                sp.wait_ge(transposed, n - 3)
                sp.wait_ge(staged[n % 2], 32 * (n // 2))
                for half in range(2):
                    sp.dma_start(stage[C * half:C * (half + 1), n % 4, :].rearrange("p (r w) -> p r w", r=2),
                                 x[1, :, HALF * half + row:HALF * half + row + 2, :]).then_inc(staged[n % 2], 16)

            sp.dma_start(const[:, :], consts).then_inc(const_loaded, 16)
            load(0, 0, 0)
            load(0, 1, 0)
            sp.dma_start(wv_raw, wv).then_inc(small_loaded, 16)
            sp.dma_start(wqk[:, 0, :], wq).then_inc(small_loaded, 16)
            sp.dma_start(wqk[:, 1, :], wk).then_inc(small_loaded, 16)
            sp.dma_start(wp_sb[:, :, :], wp.rearrange("(h d) c -> d h c", h=HEADS)).then_inc(small_loaded, 16)
            sp.dma_start(resc[:, :], rescale.rearrange("h a b -> (a b) h").broadcast_to([DH, HEADS]))\
                .then_inc(small_loaded, 16)
            for half in range(2):
                at = slice(C * half, C * (half + 1))
                sp.dma_start(taps[at, :], pos_k.rearrange("c a i j -> c (a i j)")).then_inc(small_loaded, 16)
                sp.dma_start(bp_sb[at, :], bp.rearrange("(c a) -> c a", a=1)).then_inc(small_loaded, 16)
            for k in range(2, CHUNKS):
                load(0, k, 32 * (k // 2))
            for k in range(HEAD_CHUNKS):
                load(1, k, 32 * PAIRS)

            def first_image(i):
                for number, _, e, p in pieces(0, i):
                    if isinstance(i, int) and i == 0:
                        for n in range(DIRECT_FIRST + GPP * (number and number + 1), DIRECT_FIRST + GPP * (number + 2)):
                            if n < COPIED_FIRST:
                                load_group(n)
                    store(0, i, number, e, p)
                    static = isinstance(i, int)
                    if p == 0 and not (static and not 1 <= 2 * i + e < CHUNKS - 1):
                        k = 2 * i + e + 1
                        load(1, k, 32 * (PAIRS + i + e), parity=1 - e)

            first_image(0)
            with sp.Fori(1, PAIRS - 1) as i:
                first_image(i)
            first_image(PAIRS - 1)
            with sp.Fori(0, PAIRS) as i:
                for number, _, e, p in pieces(1, i):
                    store(1, i, number, e, p)
            for parity in stored:
                for s in parity:
                    sp.wait_ge(s, STORE_INCS * B * IMAGE_PIECES // 2)

        @block.tensor
        def _(pe):
            def gram_step(n, parity, first=False):
                pe.wait_ge(staged[parity % 2], 16 * n + 32 - 16 * (parity % 2))
                wait_from(pe, xt_ready, n - 1)
                for j in range(BLOCKS):
                    last = nc.tensor.transpose(trans[:, parity % 2, P * j:P * (j + 1)],
                                               stage[:, parity, P * j:P * (j + 1)], eye)
                last.then_inc(transposed, 1)
                if not first:
                    multiply_group(n - 1, parity + 1)

            def multiply_group(n, parity):
                pe.wait_ge(xt_ready, n + 1)
                for j in range(BLOCKS):
                    v = xt[:, parity % 2, j, :]
                    nc.tensor.matmul(gram[0:C, 0:C + 1], v[:, 1:C + 1], v[:, 0:C + 1],
                                     start=False, stop=False, skip_group_check=True)
                    last = nc.tensor.matmul(gram[C:P, 0:C + 1], v[:, C + 1:P + 1], v[:, C + 1:P + 2],
                                            start=False, stop=False, skip_group_check=True)
                last.then_inc(grammed, 1)

            def add_zeros(start):
                for half in range(2):
                    last = nc.tensor.matmul(gram[C * half:C * (half + 1), 0:C + 1], ZERO_WEIGHTS, const[0:C, 0:C + 1],
                                            start=start, stop=not start, skip_group_check=True)
                return last

            def open_gram():
                add_zeros(True)

            def close_gram():
                add_zeros(False).then_inc(gram_complete, 1)

            def main(b, i, between):
                for number, first, e, p in pieces(b, i):
                    if p == 0:
                        pe.wait_ge(centred, PIECES * (b * CHUNKS + 2 * i + e + 1))
                    mine = [CENTRE] + pe_sides(has_gram(b, i), p)
                    for s in range(STRIPS):
                        wait_from(pe, acc_ready, STRIPS * (number - 2) + s + 1)
                        for dy, dx in mine:
                            o, n = span(dx)
                            w = w_mix[:, :] if (dy, dx) == CENTRE else w_side[:, SIDES.index((dy, dx)), :]
                            last = nc.tensor.matmul(conv[:, p % 2, strip(s), o], w,
                                                    rows[:, bass.ds(first + STRIP * s + dy, STRIP), n],
                                                    start=(dy, dx) == CENTRE, stop=(dy, dx) == mine[-1],
                                                    skip_group_check=True)
                        last.then_inc(conv_ready, 1)
                        between(number, e, p, s)

            def add_halves(b):
                pe.wait_ge(halves_stacked, b + 1)
                nc.tensor.matmul(BANKS[b][3][:, 0:C + 1], both, STACKED[b], start=True, stop=True)\
                    .then_inc(halves_added, 1)

            def add_groups(b):
                pe.wait_ge(diag_ready, b + 1)
                nc.tensor.matmul(BANKS[b][3][:, P:P + 2], pair, st[0:C, 0:2], start=True, stop=True)\
                    .then_inc(group_sums, 1)

            def spread_rows(b):
                pe.wait_ge(diagonals_ready, b + 1)
                nc.tensor.matmul(BANKS[b][3][0:C, 0:3 * C], ones[:, :], SCRATCH[b][0][:, 0:3 * C],
                                 start=True, stop=True).then_inc(rows_ready, 1)

            def project(b):
                pe.wait_ge(gram_normed, b + 1)
                for k in range(2):
                    last = nc.tensor.matmul(BANKS[b][k][0:C, :], NORMED[b], wqk[:, k, :], start=True, stop=True)
                last.then_inc(projected, 1)

            def norms_and_logits(b):
                pe.wait_ge(norm_terms, b + 1)
                for k in range(2):
                    for h in range(HEADS):
                        last = nc.tensor.matmul(BANKS[b][2][0:DH, HEADS * k + h:HEADS * k + h + 1],
                                                SCRATCH[b][k][:, h * DH:(h + 1) * DH], ones[:, 0:1],
                                                start=True, stop=True)
                last.then_inc(norms_ready, 1)
                for h in range(HEADS):
                    at = slice(h * DH, (h + 1) * DH)
                    last = nc.tensor.matmul(BANKS[b][0][0:DH, at], wqk[:, 1, at], SCRATCH[b][2][:, at],
                                            start=True, stop=True)
                last.then_inc(logits_ready, 1)

            def spread_query_norms(b):
                pe.wait_ge(query_diagonals, b + 1)
                nc.tensor.matmul(BANKS[b][3][0:C, :], ones[:, :], SCRATCH[b][0], start=True, stop=True)\
                    .then_inc(query_rows, 1)

            def values_out(b):
                pe.wait_ge(att_ready, b + 1)
                for h in range(HEADS):
                    at = slice(h * DH, (h + 1) * DH)
                    last = nc.tensor.matmul(BANKS[b][1][0:DH, at], SCRATCH[b][3][:, at], wp_sb[:, h, :],
                                            start=True, stop=True)
                last.then_inc(headed_ready, 1)

            def mix(b):
                pe.wait_ge(headed_copied, b + 1)
                for half in range(2):
                    for h in range(HEADS):
                        last = nc.tensor.matmul(BANKS[b][2][C * half:C * (half + 1), 0:C], wv_t[:, h, :],
                                                SCRATCH[b][1][:, h * C:(h + 1) * C], start=h == 0, stop=h == HEADS - 1)
                last.then_inc(mixing_ready, 1)

            def gram_pass(i):
                for g in range(2 * GROUPS):
                    gram_step(2 * GROUPS * i + g, g % 4, first=isinstance(i, int) and i == 0 and g == 0)

            pe.wait_ge(const_loaded, 16)
            pe.wait_ge(ones_ready, 1)
            open_gram()
            gram_pass(0)
            pe.wait_ge(small_loaded, 16 * 9)
            for h in range(HEADS):
                last = nc.tensor.transpose(misc[0:DH, C * h:C * (h + 1)], wv_raw[:, DH * h:DH * (h + 1)], eye64)
            last.then_inc(wv_transposed, 1)
            with pe.Fori(1, PAIRS) as i:
                gram_pass(i)
            multiply_group(HEAD_FIRST - 1, HEAD_FIRST - 1)
            close_gram()

            head = iter(range(HEAD_FIRST, DIRECT_FIRST))

            def head_groups(count):
                for _ in range(count):
                    n = next(head)
                    gram_step(n, n % 4, first=n == HEAD_FIRST)

            add_halves(0)
            open_gram()
            add_groups(0)
            head_groups(FILL[0])
            spread_rows(0)
            project(0)
            head_groups(FILL[1])
            norms_and_logits(0)
            head_groups(FILL[2])
            spread_query_norms(0)
            head_groups(FILL[3])
            values_out(0)
            mix(0)
            head_groups(FILL[4])
            pe.wait_ge(weights_ready, 1)

            def gram_between(number, e, p, s):
                if isinstance(number, int) and number == 0:
                    return
                gram_step(DIRECT_FIRST + GPP * (number - 1) + s, (GPP * (p - 1) + s) % 4)

            def softmax_between(number, e, p, s):
                k = PIECES * e + p
                if k == 0:
                    gram_between(number, e, p, s)
                    if s == STRIPS - 1:
                        multiply_group(ALL_GROUPS - 1, ALL_GROUPS - 1)
                        close_gram()
                for step in PE_STEPS.get(k, ()) if s == STRIPS - 1 else ():
                    {"halves": add_halves, "groups": add_groups, "rows": spread_rows, "project": project,
                     "logits": norms_and_logits, "queries": spread_query_norms, "values": values_out,
                     "mix": mix}[step](1)

            main(0, 0, gram_between)
            with pe.Fori(1, PAIRS - 1) as i:
                main(0, i, gram_between)
            main(0, PAIRS - 1, softmax_between)
            pe.wait_ge(weights_ready, 2)
            main(1, 0, lambda *_: None)
            with pe.Fori(1, PAIRS) as i:
                main(1, i, lambda *_: None)

        @block.scalar
        def _(act):
            def end_waits():
                nc.scalar.copy(tiny[:, 1:2], tiny[:, 0:1])

            def copy_out(n, parity):
                act.wait_ge(transposed, n + 1)
                wait_from(act, grammed, n - 1)
                nc.scalar.copy(xt[:, parity % 2, :, 1:P + 1],
                               trans[:, parity % 2, :].rearrange("p (j n) -> p j n", j=BLOCKS)).then_inc(xt_ready, 1)

            def centre(b, chunk, p):
                row, n = fresh(b, chunk)
                above = n - CHUNK if p == 0 else 0
                v = flat(place(b, chunk) + row + n - CHUNK + PIECE * p - above, PIECE + above)
                act.wait_ge(mean_ready, b + 1)
                nc.scalar.activation(v, v, ACT.Identity, bias=neg_mean[:, b:b + 1]).then_inc(centred, 1)

            def main(b, i, between):
                static = isinstance(i, int)
                for number, first, e, p in pieces(b, i):
                    if p == 0:
                        act.wait_ge(centred, PIECES * (b * CHUNKS + 2 * i + e + 1))
                    wait_from(act, summed, STRIPS * (number - 1))
                    wait_from(act, side_added, number)
                    end_waits()
                    nc.scalar.activation(prod[:, p % 2, :, :], flat(first + BOTTOM[0], PIECE), ACT.Identity,
                                         bias=bias[:, b:b + 1], scale=taps_a[:, b, tap(*BOTTOM):tap(*BOTTOM) + 1])\
                        .then_inc(prod_ready, 1)
                    nc.scalar.activation(side[:, :, :], flat(first + POOL_SIDE[0], PIECE), ACT.Identity,
                                         scale=taps_a[:, b, tap(*POOL_SIDE):tap(*POOL_SIDE) + 1])\
                        .then_inc(side_ready, 1)
                    between(number, e, p)
                    if not (static and (2 * i + e == CHUNKS - 1 or (b == 0 and 2 * i + e == 0))):
                        if b == 1 and p == 0:
                            act.wait_ge(loaded[1 - e], 32 * (PAIRS + i + e + 1))
                        for q in QUARTERS[p]:
                            centre(b, 2 * i + e + 1, q)

            def root_deviation(b):
                act.wait_ge(variance_ready, b + 1)
                nc.scalar.activation(dev, var, ACT.Sqrt).then_inc(deviation_ready, 1)

            def root_norms(b):
                act.wait_ge(norms_clamped, b + 1)
                nc.scalar.activation(roots[:, :, :], roots[:, :, :], ACT.Sqrt).then_inc(norms_rooted, 1)

            def exponentials(b):
                act.wait_ge(logits_shifted, b + 1)
                nc.scalar.activation(SCRATCH[b][3], SCRATCH[b][3], ACT.Exp).then_inc(exps_ready, 1)

            def gram_pass(i):
                for g in range(2 * GROUPS):
                    copy_out(2 * GROUPS * i + g, g % 4)

            act.wait_ge(ones_ready, 1)
            gram_pass(0)
            with act.Fori(1, PAIRS) as i:
                gram_pass(i)

            def stage_head(n):
                if n >= DIRECT_FIRST:
                    return
                g = n - HEAD_FIRST
                act.wait_ge(loaded[g // GROUPS], 32 * (PAIRS + 1))
                act.wait_ge(transposed, n - 3)
                nc.scalar.copy(stage[:, n % 4, :], flat(place(1, 0) + 2 * g, 2).rearrange("p r w -> p (r w)"))\
                    .then_inc(staged[n % 2], 32)

            head = iter(range(HEAD_FIRST, DIRECT_FIRST))

            def head_groups(count):
                for _ in range(count):
                    n = next(head)
                    copy_out(n, n % 4)
                    stage_head(n + 4)

            for n in range(HEAD_FIRST, HEAD_FIRST + 4):
                stage_head(n)
            root_deviation(0)
            head_groups(FILL[0])
            head_groups(FILL[1])
            root_norms(0)
            head_groups(FILL[2])
            exponentials(0)
            head_groups(FILL[3])
            head_groups(FILL[4])

            def gram_between(number, e, p):
                if isinstance(number, int) and number == 0:
                    return
                for m in range(GPP):
                    copy_out(DIRECT_FIRST + GPP * (number - 1) + m, (GPP * (p - 1) + m) % 4)

            def softmax_between(number, e, p):
                k = PIECES * e + p
                if k == 0:
                    gram_between(number, e, p)
                for step in ACT_STEPS.get(k, ()):
                    {"deviation": root_deviation, "norms": root_norms, "exp": exponentials,
                     "centre": lambda b: [centre(b, 0, q) for q in range(PIECES)]}[step](1)

            main(0, 0, gram_between)
            with act.Fori(1, PAIRS - 1) as i:
                main(0, i, gram_between)
            main(0, PAIRS - 1, softmax_between)
            main(1, 0, lambda *_: None)
            with act.Fori(1, PAIRS - 1) as i:
                main(1, i, lambda *_: None)
            main(1, PAIRS - 1, lambda *_: None)

        @block.vector
        def _(dve):
            steps = [0]

            def then(instruction):
                steps[0] += 1
                instruction.then_inc(small_step, 1)
                dve.wait_ge(small_step, steps[0])

            def stage_group(n, parity, position):
                wait_from(dve, transposed, n - 3)
                nc.vector.tensor_copy(stage[:, parity, :], flat(position, 2).rearrange("p r w -> p (r w)"))\
                    .then_inc(staged[parity % 2], 32)

            def main(b, i, between, amid):
                for number, first, e, p in pieces(b, i):
                    between(number, i, e, p)
                    if p == 0:
                        dve.wait_ge(centred, PIECES * (b * CHUNKS + 2 * i + e + 1))
                    mine = dve_sides(has_gram(b, i), p)
                    for j, (dy, dx) in enumerate(mine):
                        o, n = span(dx)
                        for s in range(STRIPS):
                            if j:
                                dve.wait_ge(tap_added, taps_before(b, i, e, p) + STRIPS * (j - 1) + s + 1)
                            else:
                                dve.wait_ge(conv_ready, STRIPS * number + s + 1)
                            v = conv[:, p % 2, strip(s), o]
                            nc.vector.scalar_tensor_tensor(out=v, in0=rows[:, bass.ds(first + STRIP * s + dy, STRIP), n],
                                                           scalar=taps_a[:, b, tap(dy, dx):tap(dy, dx) + 1], in1=v,
                                                           op0=ALU.mult, op1=ALU.add).then_inc(tap_added, 1)
                        if j == 0:
                            amid(e, p)
                    for s in range(STRIPS):
                        wait_from(dve, stored[p % 2][s],
                                  STORE_INCS * (b * IMAGE_PIECES // 2 + PIECES * i + (PIECES * e + p) // 2))
                        dve.wait_ge(tap_added, taps_before(b, i, e, p) + STRIPS * (len(mine) - 1) + s + 1)
                        nc.vector.scalar_tensor_tensor(out=acc_out[:, p % 2, strip(s), :],
                                                       in0=flat(first + STRIP * s + TOP[0], STRIP),
                                                       scalar=taps_a[:, b, tap(*TOP):tap(*TOP) + 1],
                                                       in1=conv[:, p % 2, strip(s), :],
                                                       op0=ALU.mult, op1=ALU.add).then_inc(acc_ready, 1)

            def pair_taps(gram):
                return 2 * STRIPS * sum(len(dve_sides(gram, p)) for p in range(PIECES))

            def taps_before(b, i, e, p):
                gram = has_gram(b, i)
                inner = e * pair_taps(gram) // 2 + STRIPS * sum(len(dve_sides(gram, q)) for q in range(p))
                if b == 0:
                    return pair_taps(True) * i + inner
                return pair_taps(True) * (PAIRS - 1) + pair_taps(False) * (i + 1) + inner

            def wide(v):
                return v.unsqueeze(2).broadcast_to([DH, HEADS, DH])

            def by_head(v):
                return v.rearrange("d (h e) -> d h e", h=HEADS)

            def stack_halves(b):
                dve.wait_ge(gram_complete, b + 1)
                nc.vector.tensor_copy(STACKED[b][0:C, 0:C], gram[0:C, 1:C + 1])
                nc.vector.tensor_copy(STACKED[b][0:C, C:C + 1], gram[0:C, 0:1])
                nc.vector.tensor_copy(STACKED[b][C:P, :], gram[C:P, 0:C + 1]).then_inc(halves_stacked, 1)

            def take_diagonal(b):
                dve.wait_ge(halves_added, b + 1)
                then(nc.vector.tensor_copy(GRAM[b][:, :], BANKS[b][3][:, 0:C + 1]))
                then(nc.vector.tensor_tensor(STACKED[b][:, 0:C], GRAM[b][:, 0:C], both[:, 0:C], ALU.mult))
                nc.vector.tensor_copy(sums, GRAM[b][:, C:C + 1])
                nc.vector.reduce_sum(st[:, 1:2], STACKED[b][:, 0:C], AX.X).then_inc(diag_ready, 1)

            def moments(b):
                dve.wait_ge(group_sums, b + 1)
                then(nc.vector.tensor_scalar(st[:, 2:4], BANKS[b][3][:, P:P + 2], 1.0 / (GROUP * PIX), None, ALU.mult))
                then(nc.vector.tensor_tensor(msq, mean, mean, ALU.mult))
                then(nc.vector.tensor_tensor(var, ex2, msq, ALU.subtract))
                nc.vector.tensor_scalar(var, var, 0.0, NORM_EPS, ALU.max, ALU.add).then_inc(variance_ready, 1)
                nc.vector.tensor_scalar(neg_mean[:, b:b + 1], mean, -1.0, None, ALU.mult)
                if b == 1:
                    dve.wait_ge(summed, STRIPS * (IMAGE_PIECES - 2 * PIECES + 1))
                nc.vector.tensor_scalar(rows[0:C, place(b, 0) - 1, :], const[0:C, 0:W], 0.0, mean[0:C, :],
                                        ALU.mult, ALU.add)
                nc.vector.tensor_scalar(rows[C:P, place(b, CHUNKS - 1) + HALF, :], const[C:P, 0:W], 0.0, mean[C:P, :],
                                        ALU.mult, ALU.add)
                then(nc.vector.tensor_tensor(bias[:, b:b + 1], mean, bp_sb[:, :], ALU.add))
                nc.vector.scalar_tensor_tensor(out=excess, in0=neg_mean[:, b:b + 1], scalar=float(PIX), in1=sums,
                                               op0=ALU.mult, op1=ALU.add).then_inc(mean_ready, 1)

            def scales(b):
                dve.wait_ge(mean_ready, b + 1)
                dve.wait_ge(deviation_ready, b + 1)
                then(nc.vector.reciprocal(inv, dev))
                then(nc.vector.tensor_tensor(tmp, inv, inv, ALU.mult))
                then(nc.vector.tensor_tensor(tmp, tmp, var, ALU.mult))
                then(nc.vector.tensor_scalar(tmp, tmp, -0.5, 1.5, ALU.mult, ALU.add))
                then(nc.vector.tensor_tensor(scale, inv, tmp, ALU.mult))
                for j, v in enumerate((mean, excess, scale)):
                    last = nc.vector.tensor_scalar(SCRATCH[b][0][:, C * j:C * (j + 1)], eye64, v[0:C, :], None, ALU.mult)
                last.then_inc(diagonals_ready, 1)
                nc.vector.tensor_scalar(neg_scale, scale, -1.0, None, ALU.mult)
                then(nc.vector.tensor_scalar(taps_a[:, b, :], taps[:, :], scale, None, ALU.mult))
                then(nc.vector.tensor_scalar_add(centre1, taps_a[:, b, tap(*CENTRE):tap(*CENTRE) + 1], 1.0))

            def norm_gram(b):
                dve.wait_ge(rows_ready, b + 1)
                spread = BANKS[b][3]
                then(nc.vector.scalar_tensor_tensor(out=NORMED[b], in0=spread[0:C, 0:C], scalar=st[0:C, 0:1],
                                                    in1=GRAM[b][0:C, 0:C], op0=ALU.mult, op1=ALU.subtract))
                then(nc.vector.scalar_tensor_tensor(out=NORMED[b], in0=spread[0:C, C:2 * C], scalar=mean[0:C, :],
                                                    in1=NORMED[b], op0=ALU.mult, op1=ALU.add))
                nc.vector.scalar_tensor_tensor(out=NORMED[b], in0=NORMED[b], scalar=neg_scale[0:C, :],
                                               in1=spread[0:C, 2 * C:3 * C], op0=ALU.mult, op1=ALU.mult)\
                    .then_inc(gram_normed, 1)

            def terms(b):
                dve.wait_ge(projected, b + 1)
                for k in range(2):
                    nc.vector.tensor_tensor(SCRATCH[b][k], BANKS[b][k][0:C, :], wqk[:, k, :], ALU.mult)
                nc.vector.tensor_copy(SCRATCH[b][2], BANKS[b][0][0:C, :]).then_inc(norm_terms, 1)

            def clamp_norms(b):
                dve.wait_ge(norms_ready, b + 1)
                nc.vector.tensor_scalar(roots[:, :, :].rearrange("d k h -> d (k h)"), BANKS[b][2][0:DH, 0:2 * HEADS],
                                        LEAST_SQUARE, None, ALU.max).then_inc(norms_clamped, 1)

            def invert_norms(b):
                dve.wait_ge(norms_rooted, b + 1)
                then(nc.vector.reciprocal(roots[:, :, :], roots[:, :, :]))
                nc.vector.tensor_tensor(by_head(SCRATCH[b][0]), eye64.unsqueeze(1).broadcast_to([C, HEADS, DH]),
                                        wide(roots[:, 0, :]), ALU.mult).then_inc(query_diagonals, 1)
                then(nc.vector.tensor_tensor(roots[:, 1, :], roots[:, 1, :], resc[:, :], ALU.mult))
                dve.wait_ge(logits_ready, b + 1)
                then(nc.vector.tensor_tensor(by_head(SCRATCH[b][3]), by_head(BANKS[b][0][0:C, :]),
                                             wide(roots[:, 1, :]), ALU.mult))

            def shift_logits(b):
                att = by_head(SCRATCH[b][3])
                dve.wait_ge(query_rows, b + 1)
                then(nc.vector.tensor_tensor(SCRATCH[b][3], SCRATCH[b][3], BANKS[b][3][0:C, :], ALU.mult))
                then(nc.vector.reduce_max(mx[:, :], att, AX.X))
                nc.vector.tensor_tensor(att, att, wide(mx[:, :]), ALU.subtract).then_inc(logits_shifted, 1)

            def divide(b):
                att = by_head(SCRATCH[b][3])
                dve.wait_ge(exps_ready, b + 1)
                then(nc.vector.reduce_sum(mx[:, :], att, AX.X))
                then(nc.vector.reciprocal(mx[:, :], mx[:, :]))
                nc.vector.tensor_tensor(att, att, wide(mx[:, :]), ALU.mult).then_inc(att_ready, 1)

            def copy_headed(b):
                dve.wait_ge(headed_ready, b + 1)
                nc.vector.tensor_copy(SCRATCH[b][1], BANKS[b][1][0:C, :]).then_inc(headed_copied, 1)

            def weights(b):
                dve.wait_ge(mixing_ready, b + 1)
                for half in range(2):
                    at = slice(C * half, C * (half + 1))
                    last = nc.vector.tensor_scalar(w_mix[at, at], BANKS[b][2][at, 0:C], scale[at, :], None, ALU.mult)
                then(last)
                for j, (dy, dx) in enumerate(SIDES[:2]):
                    t = tap(dy, dx)
                    nc.vector.tensor_scalar(w_side[:, j, :], eye, taps_a[:, b, t:t + 1], None, ALU.mult)
                nc.vector.scalar_tensor_tensor(out=w_mix[:, :], in0=eye, scalar=centre1, in1=w_mix[:, :],
                                               op0=ALU.mult, op1=ALU.add).then_inc(weights_ready, 1)

            ALL_STEPS = {"stack": stack_halves, "diagonal": take_diagonal, "moments": moments, "scales": scales,
                         "gram": norm_gram, "terms": terms, "clamp": clamp_norms, "invert": invert_norms,
                         "shift": shift_logits, "divide": divide, "headed": copy_headed, "weights": weights}

            nc.vector.memset(tiny[:, :], 0.0)
            nc.vector.memset(xt[:, :, :, 0:1], 1.0)
            nc.vector.memset(xt[:, :, :, P + 1:P + 2], 1.0)
            nc.vector.memset(w_mix[:, :], 0.0)
            nc.vector.memset(ones[:, :], 1.0).then_inc(ones_ready, 1)

            def gram_pass(i):
                for g in range(2 * GROUPS):
                    if isinstance(i, int) and i == 0 and g == 0:
                        dve.wait_ge(first_rows_loaded, 32)
                    if g % GROUPS == (FIRST_ROWS // 2 if isinstance(i, int) and i == 0 and g < GROUPS else 0):
                        dve.wait_ge(loaded[g // GROUPS], 32 * (i + 1))
                    stage_group(2 * GROUPS * i + g, g % 4, place(0, 0) + 2 * CHUNK * i + 2 * g)

            gram_pass(0)
            dve.wait_ge(wv_transposed, 1)
            nc.vector.tensor_copy(wv_t[:, :, :], misc[0:DH, :].rearrange("e (h c) -> e h c", h=HEADS))\
                .then_inc(wv_copied, 1)
            with dve.Fori(1, PAIRS) as i:
                gram_pass(i)
            for step in ALL_STEPS.values():
                step(0)

            def nothing(*_):
                pass

            def gram_between(number, i, e, p):
                if p == 0:
                    dve.wait_ge(loaded[e], 32 * (PAIRS + i + 1))
                for m in range(GPP):
                    stage_group(DIRECT_FIRST + GPP * number + m, (GPP * p + m) % 4,
                                place(1, HEAD_CHUNKS) + CHUNK * (2 * i + e) + 2 * (GPP * p + m))

            def softmax_amid(e, p):
                for step in DVE_STEPS.get(PIECES * e + p, ()):
                    ALL_STEPS[step](1)

            main(0, 0, nothing, nothing)
            for k in range(2):
                dve.wait_ge(staged[k], 32 * COPIED_FIRST // 2)
            with dve.Fori(1, PAIRS - 1) as i:
                main(0, i, gram_between, nothing)
            main(0, PAIRS - 1, nothing, softmax_amid)
            main(1, 0, nothing, nothing)
            with dve.Fori(1, PAIRS) as i:
                main(1, i, nothing, nothing)

        @block.gpsimd
        def _(pool):
            def main(b, i):
                for number, first, e, p in pieces(b, i):
                    o, n = span(POOL_SIDE[1])
                    v = prod[:, p % 2, :, o]
                    pool.wait_ge(prod_ready, number + 1)
                    pool.wait_ge(side_ready, number + 1)
                    nc.gpsimd.tensor_tensor(v, v, side[:, :, n], ALU.add).then_inc(side_added, 1)
                    pool.wait_ge(side_added, number + 1)
                    for s in range(STRIPS):
                        pool.wait_ge(acc_ready, STRIPS * number + s + 1)
                        v = acc_out[:, p % 2, strip(s), :]
                        nc.gpsimd.tensor_tensor(v, v, prod[:, p % 2, strip(s), :], ALU.add).then_inc(summed, 1)

            pool.wait_ge(mean_ready, 1)
            for chunk in range(2):
                row, n = fresh(0, chunk)
                v = rows[:, place(0, chunk) + row:place(0, chunk) + row + n, :]
                nc.gpsimd.tensor_scalar(v, v, neg_mean[:, 0:1], 1.0, ALU.add, ALU.mult).then_inc(centred, PIECES)
            for b in range(B):
                with pool.Fori(0, PAIRS) as i:
                    main(b, i)


_INS = ["x", "L0_conv_Wq", "L0_conv_Wk", "L0_conv_Wv", "L0_conv_rescale", "L0_conv_Wp", "L0_conv_bp", "L0_conv_pos_k"]


def _constants():
    n = np.arange(P)
    eye = n[:, None] == n[None, :]
    both = n[:, None] % C == n[None, :] % C
    pair = (n[:, None] % C) // GROUP == (n[None, :] % C) // GROUP
    return np.concatenate([eye, both, pair], axis=1).astype(np.float32)


def kernel(**inputs):
    import concourse.bacc as _bacc
    from concourse.bass_utils import run_bass_kernel_spmd as _run

    nc = _bacc.Bacc("TRN2", target_bir_lowering=False, num_devices=1)
    arrays, args = {}, []
    for name, a in [(n, inputs[n]) for n in _INS] + [("constants", _constants())]:
        a = np.ascontiguousarray(a)
        arrays[f"in_{name}"] = a
        args.append(nc.dram_tensor(f"in_{name}", a.shape, mybir.dt.from_np(a.dtype), kind="ExternalInput").ap())
    args.append(nc.dram_tensor("out_0", (B, C, H, W), F32, kind="ExternalOutput").ap())
    build(nc, *args)
    r = _run(nc, [arrays], core_ids=[0])
    return r.results[0]["out_0"]
```

```python
import numpy as np

import concourse.bass as bass
from concourse import mybir
from contextlib import ExitStack

F32 = mybir.dt.float32
ALU = mybir.AluOpType
ACT = mybir.ActivationFunctionType
AX = mybir.AxisListType

B, C, H, W = 2, 64, 256, 256
HEADS, DH = 8, 64
P = 2 * C
HALF = H // 2
PIX = H * W
GROUP = 2
NORM_EPS = 1e-5
LEAST_SQUARE = 1e-24

CHUNK = 16
CHUNKS = HALF // CHUNK
PIECE = 4
PIECES = CHUNK // PIECE
STRIP = 2
STRIPS = PIECE // STRIP
STORE_INCS = 16
PAIRS = CHUNKS // 2
IMAGE_PIECES = CHUNKS * PIECES
GROUPS = CHUNK // 2
BLOCKS = 2 * W // P
FIRST_ROWS = 4

HEAD_CHUNKS = 2
HEAD_ROWS = HEAD_CHUNKS * CHUNK + 2
ROWS = HEAD_ROWS + HALF + 2

GPP = 2
HEAD_FIRST = CHUNKS * GROUPS
DIRECT_FIRST = HEAD_FIRST + HEAD_CHUNKS * GROUPS
DIRECT_CHUNKS = (6, 7)
COPIED_FIRST = DIRECT_FIRST + len(DIRECT_CHUNKS) * GROUPS
ALL_GROUPS = 2 * CHUNKS * GROUPS
GRAM_PIECES = (ALL_GROUPS - DIRECT_FIRST) // GPP

CENTRE, TOP, BOTTOM = (0, 0), (-1, 0), (1, 0)
SIDES = [(0, -1), (0, 1), (-1, -1), (-1, 1), (1, -1), (1, 1)]
PE_SIDES = 3
POOL_SIDE = SIDES[5]


SOFTMAX_SIDES = [(1, 1), (3, 3), (2, 3), (2, 3), (2, 2), (2, 2), (3, 3), (2, 3)]


def pe_sides(beside, k, s):
    if beside == "head" and PAIR_GROUPS[k] > GPP:
        return SIDES[:1]
    if beside in ("head", "gram"):
        return SIDES[:1] if k % 2 or s else SIDES[:2]
    if beside == "softmax":
        return SIDES[:SOFTMAX_SIDES[k][s]]
    return SIDES[:2]


def dve_ops(beside, k):
    mine = [[t for t in SIDES if t not in pe_sides(beside, k, s) and t != POOL_SIDE] for s in range(STRIPS)]
    return [(s, mine[s][j]) for j in range(max(map(len, mine))) for s in range(STRIPS) if j < len(mine[s])]


def place(b, chunk):
    if b == 0:
        return HEAD_ROWS + 1
    if isinstance(chunk, int) and chunk < HEAD_CHUNKS:
        return 1
    return HEAD_ROWS - (HEAD_CHUNKS * CHUNK - 1)


def fresh(b, chunk):
    if isinstance(chunk, int) and (chunk == 0 or (b == 1 and chunk == HEAD_CHUNKS)):
        return CHUNK * chunk - 1, CHUNK + 2
    return CHUNK * chunk + 1, CHUNK


QUARTERS = [(0,), (1,), (2, 3), ()]
PAIR_GROUPS = (3, 3, 3, 2, 2, 2, 2, 2)
PAIR_FIRST = DIRECT_FIRST + GPP * (2 * PIECES - 1) - sum(PAIR_GROUPS)
FILL = (2, 1, 3, 4, 1)


def head_groups_of(number):
    first = PAIR_FIRST + sum((PAIR_GROUPS + (GPP,))[:number])
    return range(first, first + (PAIR_GROUPS + (GPP, GPP))[number])


DVE_STEPS = {(0, 1): "stack", (1, 0): "diagonal", (1, 1): "moments", (2, 1): "scales", (3, 0): "gram",
             (3, 1): "terms", (4, 0): "clamp", (4, 1): "invert", (5, 1): "shift", (6, 0): "divide",
             (6, 1): "headed", (7, 0): "weights"}
PE_STEPS = {(1, 1): "halves", (2, 0): "groups", (3, 1): "rows", (4, 0): "project", (4, 1): "logits",
            (5, 1): "queries", (7, 0): "values", (7, 1): "mix"}
ACT_STEPS = {1: "deviation", 2: "centre_above", 3: "norms", 5: "exp", 6: "centre_below"}


def tap(dy, dx):
    return 3 * (dy + 1) + dx + 1


def strip(s):
    return slice(STRIP * s, STRIP * (s + 1))


def span(d):
    return slice(max(0, -d), W - max(0, d)), slice(max(0, d), W + min(0, d))


def wait_from(eng, sem, value):
    if isinstance(value, int) and value <= 0:
        return
    eng.wait_ge(sem, value)


def build(nc, x, wq, wk, wv, rescale, wp, bp, pos_k, consts, out):
    ctx = ExitStack()
    with ctx:
        def sb(name, shape):
            return ctx.enter_context(nc.sbuf_tensor(name, shape, F32))

        def pb(name, shape):
            return ctx.enter_context(nc.psum_tensor(name, shape, F32))

        def sem(name):
            return ctx.enter_context(nc.semaphore(name))

        rows = sb("rows", [P, ROWS, W])
        stage = sb("stage", [P, 4, 512])
        xt = sb("xt", [P, 2, BLOCKS, P + 2])
        acc_out = sb("acc_out", [P, 2, PIECE, W])
        prod = sb("prod", [P, 2, PIECE, W])
        side = sb("side", [P, PIECE, W])
        const = sb("const", [P, 3 * P])
        ones = sb("ones", [C, C])
        w_mix = sb("w_mix", [P, P])
        w_side = sb("w_side", [P, PE_SIDES, P])
        wqk = sb("wqk", [C, 2, HEADS * DH])
        wp_wv = sb("wp_wv", [P, HEADS, C])
        wp_sb, wv_t = wp_wv[0:DH, :, :], wp_wv[C:P, :, :]
        taps = sb("taps", [P, 9])
        bp_sb = sb("bp_sb", [P, 1])
        resc = sb("resc", [DH, HEADS])
        taps_a = sb("taps_a", [P, B, 9])
        bias = sb("bias", [P, B])
        neg_mean = sb("neg_mean", [P, B])
        st = sb("st", [P, 16])
        roots = sb("roots", [DH, 2, HEADS])
        mx = sb("mx", [DH, HEADS])
        tiny = sb("tiny", [P, 2])

        eye = const[:, 0:P]
        both = const[:, P:2 * P]
        pair = const[0:C, 2 * P:3 * P]
        eye64 = both[0:C, 0:C]
        wv_raw = acc_out[0:C, 0, 0:2, :].rearrange("c r w -> c (r w)")
        mean, ex2, msq, var, dev, inv, tmp, scale, excess, neg_scale, centre1 = (st[:, j:j + 1] for j in range(2, 13))
        sums = st[:, 0:1]

        conv = pb("conv", [P, 2, PIECE, W])
        trans = pb("trans", [P, 2, 512])
        gram = pb("gram", [P, 512])
        misc = pb("misc", [P, 512])

        conv_banks = conv[:, :, :, :].rearrange("p n r w -> p (n r w)").rearrange("p (k c) -> p k c", k=4)
        prod_rows = prod[:, :, :, :].rearrange("p n r w -> p (n r w)").rearrange("p (k c) -> p k c", k=4)
        BANKS = [[conv_banks[:, k, :] for k in range(4)], [trans[:, 0, :], trans[:, 1, :], gram[:, :], misc[:, :]]]
        early = [prod_rows[:, 2, :], stage[:, 2, :]]
        STACKED, GRAM = [v[:, 0:C + 1] for v in early], [v[:, P:P + C + 1] for v in early]
        NORMED = [v[0:C, 2 * P:2 * P + C] for v in early]
        HEADED = [prod_rows[C:P, 1, :], stage[C:P, 1, :]]
        ZERO_WEIGHTS = w_mix[0:C, C:P]
        SCRATCH = [[prod_rows[0:C, k, :] for k in range(4)], [stage[0:C, k, :] for k in range(4)]]

        const_loaded = sem("const_loaded")
        first_rows_loaded = sem("first_rows_loaded")
        small_loaded = sem("small_loaded")
        loaded = [sem("loaded_even"), sem("loaded_odd")]
        stored = [[sem("stored_even_0"), sem("stored_even_1")], [sem("stored_odd_0"), sem("stored_odd_1")]]
        ones_ready = sem("ones_ready")
        wv_transposed = sem("wv_transposed")
        wv_copied = sem("wv_copied")
        staged = [sem("staged_even"), sem("staged_odd")]
        transposed = sem("transposed")
        xt_ready = sem("xt_ready")
        grammed = sem("grammed")
        gram_complete = sem("gram_complete")
        halves_stacked = sem("halves_stacked")
        halves_added = sem("halves_added")
        diag_ready = sem("diag_ready")
        group_sums = sem("group_sums")
        variance_ready = sem("variance_ready")
        mean_ready = sem("mean_ready")
        deviation_ready = sem("deviation_ready")
        diagonals_ready = sem("diagonals_ready")
        rows_ready = sem("rows_ready")
        gram_normed = sem("gram_normed")
        projected = sem("projected")
        norm_terms = sem("norm_terms")
        norms_ready = sem("norms_ready")
        logits_ready = sem("logits_ready")
        norms_clamped = sem("norms_clamped")
        norms_rooted = sem("norms_rooted")
        query_diagonals = sem("query_diagonals")
        query_rows = sem("query_rows")
        logits_shifted = sem("logits_shifted")
        exps_ready = sem("exps_ready")
        att_ready = sem("att_ready")
        headed_ready = sem("headed_ready")
        headed_copied = sem("headed_copied")
        mixing_ready = sem("mixing_ready")
        weights_ready = sem("weights_ready")
        small_step = sem("small_step")
        centred = sem("centred")
        conv_ready = sem("conv_ready")
        tap_added = sem("tap_added")
        acc_ready = sem("acc_ready")
        prod_ready = sem("prod_ready")
        side_ready = sem("side_ready")
        side_added = sem("side_added")
        summed = sem("summed")

        block = ctx.enter_context(nc.Block())

        def pieces(b, i):
            for e in range(2):
                for p in range(PIECES):
                    chunk = 2 * i + e
                    yield b * IMAGE_PIECES + PIECES * chunk + p, place(b, chunk) + CHUNK * chunk + PIECE * p, e, p

        def loaded_by(pair):
            return 32 * (PAIRS + 1) + 64 * pair

        def flat(first, n):
            return rows[:, bass.ds(first, n), :]

        def beside(b, i):
            if b == 1:
                return "nothing"
            return {0: "head", PAIRS - 1: "softmax"}.get(i, "gram") if isinstance(i, int) else "gram"

        @block.sync
        def _(sp):
            def load(b, k, before, parity=None, part=None):
                s = loaded[k % 2 if parity is None else parity]
                if part != 1:
                    wait_from(sp, s, before)
                row, n = fresh(b, k)
                if part == 0:
                    n -= CHUNK // 2
                if part == 1:
                    row, n = row + n - CHUNK // 2, CHUNK // 2
                edge = (isinstance(k, int) and k == 0, isinstance(k, int) and k == CHUNKS - 1)
                for half in range(2):
                    r0, m = row, n
                    if edge[0] and half == 0:
                        r0, m = r0 + 1, m - 1
                    if edge[1] and half == 1 and part != 0:
                        m -= 1
                    at = slice(C * half, C * (half + 1))
                    if b == 0 and edge[0]:
                        m0 = FIRST_ROWS - r0
                        sp.dma_start(rows[at, place(b, k) + r0:place(b, k) + r0 + m0, :],
                                     x[b, :, HALF * half + r0:HALF * half + r0 + m0, :]).then_inc(first_rows_loaded, 16)
                        r0, m = r0 + m0, m - m0
                    sp.dma_start(rows[at, bass.ds(place(b, k) + r0, m), :],
                                 x[b, :, bass.ds(HALF * half + r0, m), :]).then_inc(s, 16)

            def store(b, i, number, e, p):
                for s in range(STRIPS):
                    sp.wait_ge(summed, STRIPS * number + s + 1)
                    row = CHUNK * (2 * i + e) + PIECE * p + STRIP * s
                    sp.dma_start(out[b].rearrange("c (h r) w -> h c r w", h=2)[:, :, bass.ds(row, STRIP), :],
                                 acc_out[:, p % 2, strip(s), :]).then_inc(stored[p % 2][s], 16)

            def load_group(n):
                chunk = DIRECT_CHUNKS[(n - DIRECT_FIRST) // GROUPS]
                row = CHUNK * chunk + 2 * ((n - DIRECT_FIRST) % GROUPS)
                sp.wait_ge(transposed, n - 3)
                sp.wait_ge(staged[n % 2], 32 * (n // 2))
                for half in range(2):
                    sp.dma_start(stage[C * half:C * (half + 1), n % 4, :].rearrange("p (r w) -> p r w", r=2),
                                 x[1, :, HALF * half + row:HALF * half + row + 2, :]).then_inc(staged[n % 2], 16)

            sp.dma_start(const[:, :], consts).then_inc(const_loaded, 16)
            load(0, 0, 0)
            load(0, 1, 0)
            sp.dma_start(wv_raw, wv).then_inc(small_loaded, 16)
            sp.dma_start(wqk[:, 0, :], wq).then_inc(small_loaded, 16)
            sp.dma_start(wqk[:, 1, :], wk).then_inc(small_loaded, 16)
            sp.dma_start(wp_sb[:, :, :], wp.rearrange("(h d) c -> d h c", h=HEADS)).then_inc(small_loaded, 16)
            sp.dma_start(resc[:, :], rescale.rearrange("h a b -> (a b) h").broadcast_to([DH, HEADS]))\
                .then_inc(small_loaded, 16)
            for half in range(2):
                at = slice(C * half, C * (half + 1))
                sp.dma_start(taps[at, :], pos_k.rearrange("c a i j -> c (a i j)")).then_inc(small_loaded, 16)
                sp.dma_start(bp_sb[at, :], bp.rearrange("(c a) -> c a", a=1)).then_inc(small_loaded, 16)
            for k in range(2, CHUNKS):
                load(0, k, 32 * (k // 2))
            for k in range(HEAD_CHUNKS):
                load(1, k, 32 * PAIRS)

            def first_image(i):
                for number, _, e, p in pieces(0, i):
                    if isinstance(i, int) and i == 0:
                        for k in range(3) if number == 0 else (number + 2,):
                            for n in head_groups_of(k):
                                if DIRECT_FIRST <= n < COPIED_FIRST:
                                    load_group(n)
                    store(0, i, number, e, p)
                    static = isinstance(i, int)
                    if p < 2 and not (static and not 1 <= 2 * i + e < CHUNKS - 1):
                        load(1, 2 * i + e + 1, loaded_by(i + e - 1), parity=1 - e, part=p)

            first_image(0)
            with sp.Fori(1, PAIRS - 1) as i:
                first_image(i)
            first_image(PAIRS - 1)
            with sp.Fori(0, PAIRS) as i:
                for number, _, e, p in pieces(1, i):
                    store(1, i, number, e, p)
            for parity in stored:
                for s in parity:
                    sp.wait_ge(s, STORE_INCS * B * IMAGE_PIECES // 2)

        @block.tensor
        def _(pe):
            def gram_step(n, parity, first=False):
                pe.wait_ge(staged[parity % 2], 16 * n + 32 - 16 * (parity % 2))
                wait_from(pe, xt_ready, n - 1)
                for j in range(BLOCKS):
                    last = nc.tensor.transpose(trans[:, parity % 2, P * j:P * (j + 1)],
                                               stage[:, parity, P * j:P * (j + 1)], eye)
                last.then_inc(transposed, 1)
                if not first:
                    multiply_group(n - 1, parity + 1)

            def multiply_group(n, parity):
                pe.wait_ge(xt_ready, n + 1)
                for j in range(BLOCKS):
                    v = xt[:, parity % 2, j, :]
                    nc.tensor.matmul(gram[0:C, 0:C + 1], v[:, 1:C + 1], v[:, 0:C + 1],
                                     start=False, stop=False, skip_group_check=True)
                    last = nc.tensor.matmul(gram[C:P, 0:C + 1], v[:, C + 1:P + 1], v[:, C + 1:P + 2],
                                            start=False, stop=False, skip_group_check=True)
                last.then_inc(grammed, 1)

            def add_zeros(start):
                for half in range(2):
                    last = nc.tensor.matmul(gram[C * half:C * (half + 1), 0:C + 1], ZERO_WEIGHTS, const[0:C, 0:C + 1],
                                            start=start, stop=not start, skip_group_check=True)
                return last

            def open_gram():
                add_zeros(True)

            def close_gram():
                add_zeros(False).then_inc(gram_complete, 1)

            def main(b, i, between):
                for number, first, e, p in pieces(b, i):
                    if p == 0:
                        pe.wait_ge(centred, PIECES * (b * CHUNKS + 2 * i + e + 1))
                    for s in range(STRIPS):
                        mine = [CENTRE] + pe_sides(beside(b, i), PIECES * e + p, s)
                        wait_from(pe, acc_ready, STRIPS * (number - 2) + s + 1)
                        for dy, dx in mine:
                            o, n = span(dx)
                            w = w_mix[:, :] if (dy, dx) == CENTRE else w_side[:, SIDES.index((dy, dx)), :]
                            last = nc.tensor.matmul(conv[:, p % 2, strip(s), o], w,
                                                    rows[:, bass.ds(first + STRIP * s + dy, STRIP), n],
                                                    start=(dy, dx) == CENTRE, stop=(dy, dx) == mine[-1],
                                                    skip_group_check=True)
                        last.then_inc(conv_ready, 1)
                        between(number, e, p, s)

            def add_halves(b):
                pe.wait_ge(halves_stacked, b + 1)
                nc.tensor.matmul(BANKS[b][3][:, 0:C + 1], both, STACKED[b], start=True, stop=True)\
                    .then_inc(halves_added, 1)

            def add_groups(b):
                pe.wait_ge(diag_ready, b + 1)
                nc.tensor.matmul(BANKS[b][3][:, P:P + 2], pair, st[0:C, 0:2], start=True, stop=True)\
                    .then_inc(group_sums, 1)

            def spread_rows(b):
                pe.wait_ge(diagonals_ready, b + 1)
                nc.tensor.matmul(BANKS[b][3][0:C, 0:3 * C], ones[:, :], SCRATCH[b][0][:, 0:3 * C],
                                 start=True, stop=True).then_inc(rows_ready, 1)

            def project(b):
                pe.wait_ge(gram_normed, b + 1)
                for k in range(2):
                    last = nc.tensor.matmul(BANKS[b][k][0:C, :], NORMED[b], wqk[:, k, :], start=True, stop=True)
                last.then_inc(projected, 1)

            def norms_and_logits(b):
                pe.wait_ge(norm_terms, b + 1)
                for k in range(2):
                    for h in range(HEADS):
                        last = nc.tensor.matmul(BANKS[b][2][0:DH, HEADS * k + h:HEADS * k + h + 1],
                                                SCRATCH[b][k][:, h * DH:(h + 1) * DH], ones[:, 0:1],
                                                start=True, stop=True)
                last.then_inc(norms_ready, 1)
                for h in range(HEADS):
                    at = slice(h * DH, (h + 1) * DH)
                    last = nc.tensor.matmul(BANKS[b][0][0:DH, at], wqk[:, 1, at], SCRATCH[b][2][:, at],
                                            start=True, stop=True)
                last.then_inc(logits_ready, 1)

            def spread_query_norms(b):
                pe.wait_ge(query_diagonals, b + 1)
                nc.tensor.matmul(BANKS[b][3][0:C, :], ones[:, :], SCRATCH[b][0], start=True, stop=True)\
                    .then_inc(query_rows, 1)

            def values_out(b):
                pe.wait_ge(att_ready, b + 1)
                for h in range(HEADS):
                    at = slice(h * DH, (h + 1) * DH)
                    last = nc.tensor.matmul(BANKS[b][1][C:P, at], SCRATCH[b][3][:, at], wp_sb[:, h, :],
                                            start=True, stop=True)
                last.then_inc(headed_ready, 1)

            def mix(b):
                pe.wait_ge(headed_copied, b + 1)
                for half in range(2):
                    for h in range(HEADS):
                        last = nc.tensor.matmul(BANKS[b][2][C * half:C * (half + 1), 0:C], wv_t[:, h, :],
                                                HEADED[b][:, h * C:(h + 1) * C], start=h == 0, stop=h == HEADS - 1)
                last.then_inc(mixing_ready, 1)

            def gram_pass(i):
                for g in range(2 * GROUPS):
                    gram_step(2 * GROUPS * i + g, g % 4, first=isinstance(i, int) and i == 0 and g == 0)

            pe.wait_ge(const_loaded, 16)
            pe.wait_ge(ones_ready, 1)
            open_gram()
            gram_pass(0)
            pe.wait_ge(small_loaded, 16 * 9)
            for h in range(HEADS):
                last = nc.tensor.matmul(misc[C:P, C * h:C * (h + 1)], wv_raw[:, DH * h:DH * (h + 1)], eye64,
                                        start=True, stop=True)
            last.then_inc(wv_transposed, 1)
            with pe.Fori(1, PAIRS) as i:
                gram_pass(i)
            multiply_group(HEAD_FIRST - 1, HEAD_FIRST - 1)
            close_gram()

            head = iter(range(HEAD_FIRST, DIRECT_FIRST))

            def head_groups(count):
                for _ in range(count):
                    n = next(head)
                    gram_step(n, n % 4, first=n == HEAD_FIRST)

            add_halves(0)
            open_gram()
            add_groups(0)
            head_groups(FILL[0])
            spread_rows(0)
            project(0)
            head_groups(FILL[1])
            norms_and_logits(0)
            head_groups(FILL[2])
            spread_query_norms(0)
            head_groups(FILL[3])
            values_out(0)
            mix(0)
            head_groups(FILL[4])
            pe.wait_ge(weights_ready, 1)

            def head_between(number, e, p, s):
                for n in head_groups_of(number)[slice(0, 1) if s == 0 else slice(1, None)]:
                    gram_step(n, n % 4)

            def gram_between(number, e, p, s):
                gram_step(DIRECT_FIRST + GPP * (number - 1) + s, (GPP * (p - 1) + s) % 4)

            def softmax_between(number, e, p, s):
                k = PIECES * e + p
                if k == 0:
                    gram_between(number, e, p, s)
                    if s == STRIPS - 1:
                        multiply_group(ALL_GROUPS - 1, ALL_GROUPS - 1)
                        close_gram()
                step = PE_STEPS.get((k, s))
                if step:
                    {"halves": add_halves, "groups": add_groups, "rows": spread_rows, "project": project,
                     "logits": norms_and_logits, "queries": spread_query_norms, "values": values_out,
                     "mix": mix}[step](1)

            main(0, 0, head_between)
            with pe.Fori(1, PAIRS - 1) as i:
                main(0, i, gram_between)
            main(0, PAIRS - 1, softmax_between)
            pe.wait_ge(weights_ready, 2)
            main(1, 0, lambda *_: None)
            with pe.Fori(1, PAIRS) as i:
                main(1, i, lambda *_: None)

        @block.scalar
        def _(act):
            def nothing(*_):
                pass

            def end_waits():
                nc.scalar.copy(tiny[:, 1:2], tiny[:, 0:1])

            def copy_out(n, parity):
                act.wait_ge(transposed, n + 1)
                wait_from(act, grammed, n - 1)
                nc.scalar.copy(xt[:, parity % 2, :, 1:P + 1],
                               trans[:, parity % 2, :].rearrange("p (j n) -> p j n", j=BLOCKS)).then_inc(xt_ready, 1)

            def centre(b, chunk, p):
                row, n = fresh(b, chunk)
                above = n - CHUNK if p == 0 else 0
                v = flat(place(b, chunk) + row + n - CHUNK + PIECE * p - above, PIECE + above)
                act.wait_ge(mean_ready, b + 1)
                nc.scalar.activation(v, v, ACT.Identity, bias=neg_mean[:, b:b + 1]).then_inc(centred, 1)

            def main(b, i, before=nothing, after=nothing):
                static = isinstance(i, int)
                for number, first, e, p in pieces(b, i):
                    before(number, e, p)
                    if p == 0:
                        act.wait_ge(centred, PIECES * (b * CHUNKS + 2 * i + e + 1))
                    wait_from(act, summed, STRIPS * (number - 1))
                    wait_from(act, side_added, number)
                    copied = beside(b, i) == "gram"
                    if copied:
                        group = DIRECT_FIRST + GPP * number
                        act.wait_ge(transposed, group + GPP - 4)
                        if p == 0:
                            act.wait_ge(loaded[e], loaded_by(i))
                    end_waits()
                    if copied:
                        for m in range(GPP):
                            row = place(1, HEAD_CHUNKS) + CHUNK * (2 * i + e) + 2 * (GPP * p + m)
                            nc.scalar.copy(stage[:, (GPP * p + m) % 4, :], flat(row, 2).rearrange("p r w -> p (r w)"))\
                                .then_inc(staged[m % 2], 32)
                    nc.scalar.activation(prod[:, p % 2, :, :], flat(first + BOTTOM[0], PIECE), ACT.Identity,
                                         bias=bias[:, b:b + 1], scale=taps_a[:, b, tap(*BOTTOM):tap(*BOTTOM) + 1])\
                        .then_inc(prod_ready, 1)
                    nc.scalar.activation(side[:, :, :], flat(first + POOL_SIDE[0], PIECE), ACT.Identity,
                                         scale=taps_a[:, b, tap(*POOL_SIDE):tap(*POOL_SIDE) + 1])\
                        .then_inc(side_ready, 1)
                    if not (static and (2 * i + e == CHUNKS - 1 or (b == 0 and 2 * i + e == 0))):
                        if b == 1 and p == 0:
                            act.wait_ge(loaded[1 - e], loaded_by(i + e))
                        for q in QUARTERS[p]:
                            centre(b, 2 * i + e + 1, q)
                    after(number, e, p)

            def root_deviation(b):
                act.wait_ge(variance_ready, b + 1)
                nc.scalar.activation(dev, var, ACT.Sqrt).then_inc(deviation_ready, 1)

            def root_norms(b):
                act.wait_ge(norms_clamped, b + 1)
                nc.scalar.activation(roots[:, :, :], roots[:, :, :], ACT.Sqrt).then_inc(norms_rooted, 1)

            def exponentials(b):
                act.wait_ge(logits_shifted, b + 1)
                nc.scalar.activation(SCRATCH[b][3], SCRATCH[b][3], ACT.Exp).then_inc(exps_ready, 1)

            def gram_pass(i):
                for g in range(2 * GROUPS):
                    copy_out(2 * GROUPS * i + g, g % 4)

            act.wait_ge(ones_ready, 1)
            gram_pass(0)
            with act.Fori(1, PAIRS) as i:
                gram_pass(i)

            def stage_head(n):
                if n >= DIRECT_FIRST:
                    return
                g = n - HEAD_FIRST
                act.wait_ge(loaded[g // GROUPS], 32 * (PAIRS + 1))
                act.wait_ge(transposed, n - 3)
                nc.scalar.copy(stage[:, n % 4, :], flat(place(1, 0) + 2 * g, 2).rearrange("p r w -> p (r w)"))\
                    .then_inc(staged[n % 2], 32)

            head = iter(range(HEAD_FIRST, DIRECT_FIRST))

            def head_groups(count):
                for _ in range(count):
                    n = next(head)
                    copy_out(n, n % 4)
                    stage_head(n + 4)

            for n in range(HEAD_FIRST, HEAD_FIRST + 4):
                stage_head(n)
            root_deviation(0)
            head_groups(FILL[0])
            head_groups(FILL[1])
            root_norms(0)
            head_groups(FILL[2])
            exponentials(0)
            head_groups(FILL[3])
            head_groups(FILL[4])

            def head_between(number, e, p):
                for n in head_groups_of(number):
                    copy_out(n, n % 4)
                    stage_head(n + 4)

            def gram_between(number, e, p):
                for m in range(GPP):
                    copy_out(DIRECT_FIRST + GPP * (number - 1) + m, (GPP * (p - 1) + m) % 4)

            def last_between(number, e, p):
                if PIECES * e + p == 0:
                    gram_between(number, e, p)

            def softmax_between(number, e, p):
                k = PIECES * e + p
                step = ACT_STEPS.get(k)
                if step:
                    {"deviation": root_deviation, "norms": root_norms, "exp": exponentials,
                     "centre_above": lambda b: [centre(b, 0, q) for q in range(2)],
                     "centre_below": lambda b: [centre(b, 0, q) for q in range(2, 4)]}[step](1)

            main(0, 0, head_between)
            for k in range(2):
                act.wait_ge(staged[k], 32 * COPIED_FIRST // 2)
            with act.Fori(1, PAIRS - 1) as i:
                main(0, i, gram_between)
            main(0, PAIRS - 1, last_between, softmax_between)
            main(1, 0)
            with act.Fori(1, PAIRS - 1) as i:
                main(1, i)
            main(1, PAIRS - 1)

        @block.vector
        def _(dve):
            steps = [0]

            def then(instruction):
                steps[0] += 1
                instruction.then_inc(small_step, 1)
                dve.wait_ge(small_step, steps[0])

            def stage_group(n, parity, position):
                wait_from(dve, transposed, n - 3)
                nc.vector.tensor_copy(stage[:, parity, :], flat(position, 2).rearrange("p r w -> p (r w)"))\
                    .then_inc(staged[parity % 2], 32)

            def main(b, i, amid):
                for number, first, e, p in pieces(b, i):
                    if p == 0:
                        dve.wait_ge(centred, PIECES * (b * CHUNKS + 2 * i + e + 1))
                    ops = dve_ops(beside(b, i), PIECES * e + p)
                    through = [0] * STRIPS
                    for m, (s, (dy, dx)) in enumerate(ops):
                        if through[s]:
                            dve.wait_ge(tap_added, taps_before(b, i, e, p) + through[s])
                        else:
                            dve.wait_ge(conv_ready, STRIPS * number + s + 1)
                        o, n = span(dx)
                        v = conv[:, p % 2, strip(s), o]
                        nc.vector.scalar_tensor_tensor(out=v, in0=rows[:, bass.ds(first + STRIP * s + dy, STRIP), n],
                                                       scalar=taps_a[:, b, tap(dy, dx):tap(dy, dx) + 1], in1=v,
                                                       op0=ALU.mult, op1=ALU.add).then_inc(tap_added, 1)
                        through[s] = m + 1
                        if m + 1 in (STRIPS, len(ops)):
                            amid(e, p, m + 1 == len(ops))
                    for s in range(STRIPS):
                        wait_from(dve, stored[p % 2][s],
                                  STORE_INCS * (b * IMAGE_PIECES // 2 + PIECES * i + (PIECES * e + p) // 2))
                        dve.wait_ge(tap_added, taps_before(b, i, e, p) + through[s])
                        nc.vector.scalar_tensor_tensor(out=acc_out[:, p % 2, strip(s), :],
                                                       in0=flat(first + STRIP * s + TOP[0], STRIP),
                                                       scalar=taps_a[:, b, tap(*TOP):tap(*TOP) + 1],
                                                       in1=conv[:, p % 2, strip(s), :],
                                                       op0=ALU.mult, op1=ALU.add).then_inc(acc_ready, 1)

            def pair_taps(what):
                return sum(len(dve_ops(what, k)) for k in range(2 * PIECES))

            def taps_before(b, i, e, p):
                what = beside(b, i)
                inner = sum(len(dve_ops(what, k)) for k in range(PIECES * e + p))
                if b == 0:
                    return inner if what == "head" else pair_taps("head") + pair_taps("gram") * (i - 1) + inner
                return pair_taps("head") + pair_taps("gram") * (PAIRS - 2) + pair_taps("softmax") + pair_taps("nothing") * i + inner

            def wide(v):
                return v.unsqueeze(2).broadcast_to([DH, HEADS, DH])

            def by_head(v):
                return v.rearrange("d (h e) -> d h e", h=HEADS)

            def stack_halves(b):
                dve.wait_ge(gram_complete, b + 1)
                nc.vector.tensor_copy(STACKED[b][0:C, 0:C], gram[0:C, 1:C + 1])
                nc.vector.tensor_copy(STACKED[b][0:C, C:C + 1], gram[0:C, 0:1])
                nc.vector.tensor_copy(STACKED[b][C:P, :], gram[C:P, 0:C + 1]).then_inc(halves_stacked, 1)

            def take_diagonal(b):
                dve.wait_ge(halves_added, b + 1)
                then(nc.vector.tensor_copy(GRAM[b][:, :], BANKS[b][3][:, 0:C + 1]))
                then(nc.vector.tensor_tensor(STACKED[b][:, 0:C], GRAM[b][:, 0:C], both[:, 0:C], ALU.mult))
                nc.vector.tensor_copy(sums, GRAM[b][:, C:C + 1])
                nc.vector.reduce_sum(st[:, 1:2], STACKED[b][:, 0:C], AX.X).then_inc(diag_ready, 1)

            def moments(b):
                dve.wait_ge(group_sums, b + 1)
                then(nc.vector.tensor_scalar(st[:, 2:4], BANKS[b][3][:, P:P + 2], 1.0 / (GROUP * PIX), None, ALU.mult))
                then(nc.vector.tensor_tensor(msq, mean, mean, ALU.mult))
                then(nc.vector.tensor_tensor(var, ex2, msq, ALU.subtract))
                nc.vector.tensor_scalar(var, var, 0.0, NORM_EPS, ALU.max, ALU.add).then_inc(variance_ready, 1)
                nc.vector.tensor_scalar(neg_mean[:, b:b + 1], mean, -1.0, None, ALU.mult)
                if b == 1:
                    dve.wait_ge(summed, STRIPS * (IMAGE_PIECES - 2 * PIECES + 1))
                nc.vector.tensor_scalar(rows[0:C, place(b, 0) - 1, :], const[0:C, 0:W], 0.0, mean[0:C, :],
                                        ALU.mult, ALU.add)
                nc.vector.tensor_scalar(rows[C:P, place(b, CHUNKS - 1) + HALF, :], const[C:P, 0:W], 0.0, mean[C:P, :],
                                        ALU.mult, ALU.add)
                then(nc.vector.tensor_tensor(bias[:, b:b + 1], mean, bp_sb[:, :], ALU.add))
                nc.vector.scalar_tensor_tensor(out=excess, in0=neg_mean[:, b:b + 1], scalar=float(PIX), in1=sums,
                                               op0=ALU.mult, op1=ALU.add).then_inc(mean_ready, 1)

            def scales(b):
                dve.wait_ge(mean_ready, b + 1)
                dve.wait_ge(deviation_ready, b + 1)
                then(nc.vector.reciprocal(inv, dev))
                then(nc.vector.tensor_tensor(tmp, inv, inv, ALU.mult))
                then(nc.vector.tensor_tensor(tmp, tmp, var, ALU.mult))
                then(nc.vector.tensor_scalar(tmp, tmp, -0.5, 1.5, ALU.mult, ALU.add))
                then(nc.vector.tensor_tensor(scale, inv, tmp, ALU.mult))
                for j, v in enumerate((mean, excess, scale)):
                    last = nc.vector.tensor_scalar(SCRATCH[b][0][:, C * j:C * (j + 1)], eye64, v[0:C, :], None, ALU.mult)
                last.then_inc(diagonals_ready, 1)
                nc.vector.tensor_scalar(neg_scale, scale, -1.0, None, ALU.mult)
                then(nc.vector.tensor_scalar(taps_a[:, b, :], taps[:, :], scale, None, ALU.mult))
                then(nc.vector.tensor_scalar_add(centre1, taps_a[:, b, tap(*CENTRE):tap(*CENTRE) + 1], 1.0))

            def norm_gram(b):
                dve.wait_ge(rows_ready, b + 1)
                spread = BANKS[b][3]
                then(nc.vector.scalar_tensor_tensor(out=NORMED[b], in0=spread[0:C, 0:C], scalar=st[0:C, 0:1],
                                                    in1=GRAM[b][0:C, 0:C], op0=ALU.mult, op1=ALU.subtract))
                then(nc.vector.scalar_tensor_tensor(out=NORMED[b], in0=spread[0:C, C:2 * C], scalar=mean[0:C, :],
                                                    in1=NORMED[b], op0=ALU.mult, op1=ALU.add))
                nc.vector.scalar_tensor_tensor(out=NORMED[b], in0=NORMED[b], scalar=neg_scale[0:C, :],
                                               in1=spread[0:C, 2 * C:3 * C], op0=ALU.mult, op1=ALU.mult)\
                    .then_inc(gram_normed, 1)

            def terms(b):
                dve.wait_ge(projected, b + 1)
                for k in range(2):
                    nc.vector.tensor_tensor(SCRATCH[b][k], BANKS[b][k][0:C, :], wqk[:, k, :], ALU.mult)
                nc.vector.tensor_copy(SCRATCH[b][2], BANKS[b][0][0:C, :]).then_inc(norm_terms, 1)

            def clamp_norms(b):
                dve.wait_ge(norms_ready, b + 1)
                nc.vector.tensor_scalar(roots[:, :, :].rearrange("d k h -> d (k h)"), BANKS[b][2][0:DH, 0:2 * HEADS],
                                        LEAST_SQUARE, None, ALU.max).then_inc(norms_clamped, 1)

            def invert_norms(b):
                dve.wait_ge(norms_rooted, b + 1)
                then(nc.vector.reciprocal(roots[:, :, :], roots[:, :, :]))
                nc.vector.tensor_tensor(by_head(SCRATCH[b][0]), eye64.unsqueeze(1).broadcast_to([C, HEADS, DH]),
                                        wide(roots[:, 0, :]), ALU.mult).then_inc(query_diagonals, 1)
                then(nc.vector.tensor_tensor(roots[:, 1, :], roots[:, 1, :], resc[:, :], ALU.mult))
                dve.wait_ge(logits_ready, b + 1)
                then(nc.vector.tensor_tensor(by_head(SCRATCH[b][3]), by_head(BANKS[b][0][0:C, :]),
                                             wide(roots[:, 1, :]), ALU.mult))

            def shift_logits(b):
                att = by_head(SCRATCH[b][3])
                dve.wait_ge(query_rows, b + 1)
                then(nc.vector.tensor_tensor(SCRATCH[b][3], SCRATCH[b][3], BANKS[b][3][0:C, :], ALU.mult))
                then(nc.vector.reduce_max(mx[:, :], att, AX.X))
                nc.vector.tensor_tensor(att, att, wide(mx[:, :]), ALU.subtract).then_inc(logits_shifted, 1)

            def divide(b):
                att = by_head(SCRATCH[b][3])
                dve.wait_ge(exps_ready, b + 1)
                then(nc.vector.reduce_sum(mx[:, :], att, AX.X))
                then(nc.vector.reciprocal(mx[:, :], mx[:, :]))
                nc.vector.tensor_tensor(att, att, wide(mx[:, :]), ALU.mult).then_inc(att_ready, 1)

            def copy_headed(b):
                dve.wait_ge(headed_ready, b + 1)
                nc.vector.tensor_copy(HEADED[b], BANKS[b][1][C:P, :]).then_inc(headed_copied, 1)

            def weights(b):
                dve.wait_ge(mixing_ready, b + 1)
                for half in range(2):
                    at = slice(C * half, C * (half + 1))
                    last = nc.vector.tensor_scalar(w_mix[at, at], BANKS[b][2][at, 0:C], scale[at, :], None, ALU.mult)
                then(last)
                for j, (dy, dx) in enumerate(SIDES[:PE_SIDES]):
                    t = tap(dy, dx)
                    nc.vector.tensor_scalar(w_side[:, j, :], eye, taps_a[:, b, t:t + 1], None, ALU.mult)
                nc.vector.scalar_tensor_tensor(out=w_mix[:, :], in0=eye, scalar=centre1, in1=w_mix[:, :],
                                               op0=ALU.mult, op1=ALU.add).then_inc(weights_ready, 1)

            ALL_STEPS = {"stack": stack_halves, "diagonal": take_diagonal, "moments": moments, "scales": scales,
                         "gram": norm_gram, "terms": terms, "clamp": clamp_norms, "invert": invert_norms,
                         "shift": shift_logits, "divide": divide, "headed": copy_headed, "weights": weights}

            nc.vector.memset(tiny[:, :], 0.0)
            nc.vector.memset(xt[:, :, :, 0:1], 1.0)
            nc.vector.memset(xt[:, :, :, P + 1:P + 2], 1.0)
            nc.vector.memset(w_mix[:, :], 0.0)
            nc.vector.memset(ones[:, :], 1.0).then_inc(ones_ready, 1)

            def gram_pass(i):
                for g in range(2 * GROUPS):
                    if isinstance(i, int) and i == 0 and g == 0:
                        dve.wait_ge(first_rows_loaded, 32)
                    if g % GROUPS == (FIRST_ROWS // 2 if isinstance(i, int) and i == 0 and g < GROUPS else 0):
                        dve.wait_ge(loaded[g // GROUPS], 32 * (i + 1))
                    stage_group(2 * GROUPS * i + g, g % 4, place(0, 0) + 2 * CHUNK * i + 2 * g)

            gram_pass(0)
            dve.wait_ge(wv_transposed, 1)
            nc.vector.tensor_copy(wv_t[:, :, :], misc[C:P, :].rearrange("e (h c) -> e h c", h=HEADS))\
                .then_inc(wv_copied, 1)
            with dve.Fori(1, PAIRS) as i:
                gram_pass(i)
            for step in ALL_STEPS.values():
                step(0)

            def nothing(*_):
                pass

            def softmax_amid(e, p, last):
                step = DVE_STEPS.get((PIECES * e + p, int(last)))
                if step:
                    ALL_STEPS[step](1)

            main(0, 0, nothing)
            with dve.Fori(1, PAIRS - 1) as i:
                main(0, i, nothing)
            main(0, PAIRS - 1, softmax_amid)
            main(1, 0, nothing)
            with dve.Fori(1, PAIRS) as i:
                main(1, i, nothing)

        @block.gpsimd
        def _(pool):
            def main(b, i):
                for number, first, e, p in pieces(b, i):
                    o, n = span(POOL_SIDE[1])
                    v = prod[:, p % 2, :, o]
                    pool.wait_ge(prod_ready, number + 1)
                    pool.wait_ge(side_ready, number + 1)
                    nc.gpsimd.tensor_tensor(v, v, side[:, :, n], ALU.add).then_inc(side_added, 1)
                    pool.wait_ge(side_added, number + 1)
                    for s in range(STRIPS):
                        pool.wait_ge(acc_ready, STRIPS * number + s + 1)
                        v = acc_out[:, p % 2, strip(s), :]
                        nc.gpsimd.tensor_tensor(v, v, prod[:, p % 2, strip(s), :], ALU.add).then_inc(summed, 1)

            pool.wait_ge(mean_ready, 1)
            for chunk in range(2):
                row, n = fresh(0, chunk)
                v = rows[:, place(0, chunk) + row:place(0, chunk) + row + n, :]
                nc.gpsimd.tensor_scalar(v, v, neg_mean[:, 0:1], 1.0, ALU.add, ALU.mult).then_inc(centred, PIECES)
            for b in range(B):
                with pool.Fori(0, PAIRS) as i:
                    main(b, i)


_INS = ["x", "L0_conv_Wq", "L0_conv_Wk", "L0_conv_Wv", "L0_conv_rescale", "L0_conv_Wp", "L0_conv_bp", "L0_conv_pos_k"]


def _constants():
    n = np.arange(P)
    eye = n[:, None] == n[None, :]
    both = n[:, None] % C == n[None, :] % C
    pair = (n[:, None] % C) // GROUP == (n[None, :] % C) // GROUP
    return np.concatenate([eye, both, pair], axis=1).astype(np.float32)


def kernel(**inputs):
    import concourse.bacc as _bacc
    from concourse.bass_utils import run_bass_kernel_spmd as _run

    nc = _bacc.Bacc("TRN2", target_bir_lowering=False, num_devices=1)
    arrays, args = {}, []
    for name, a in [(n, inputs[n]) for n in _INS] + [("constants", _constants())]:
        a = np.ascontiguousarray(a)
        arrays[f"in_{name}"] = a
        args.append(nc.dram_tensor(f"in_{name}", a.shape, mybir.dt.from_np(a.dtype), kind="ExternalInput").ap())
    args.append(nc.dram_tensor("out_0", (B, C, H, W), F32, kind="ExternalOutput").ap())
    build(nc, *args)
    r = _run(nc, [arrays], core_ids=[0])
    return r.results[0]["out_0"]
```
